# Optimizing a Trainium2 kernel written in Bass

```python
import numpy as np
import jax
import jax.numpy as jnp

def _softmax(x, axis=-1):
    return jax.nn.softmax(x, axis=axis)

def _gelu(x):
    return jax.nn.gelu(x, approximate=True)

def _silu(x):
    return jax.nn.silu(x)

def _sigmoid(x):
    return jax.nn.sigmoid(x)

def _layernorm(x, axis=-1, eps=1e-05):
    m = jnp.mean(x, axis=axis, keepdims=True)
    v = jnp.var(x, axis=axis, keepdims=True)
    return (x - m) / jnp.sqrt(v + eps)

def _scatter_add(tgt, idx, src, axis=0):
    return tgt.at[idx].add(src)

def _segment_sum(src, seg, n):
    return jax.ops.segment_sum(src, seg, n)
kernel_name = 'mk_flamingo_gated_d1_seqx_r2_970b48'

def setup_inputs(seed: int=0):
    np.random.seed(seed)
    _w = jnp.asarray

    def _rec_inputs():
        import jax
        import jax.numpy as jnp
        _rk = jax.random.key(seed)
        x = -0.0003929 + 0.9999 * jax.random.normal(jax.random.fold_in(_rk, 1), (2, 2048, 512), jnp.float32)
        _lenS = 2048 - jax.random.randint(jax.random.fold_in(_rk, 7), (2,), 0, max(1, 2048 // 4) + 1, jnp.int32)
        _lenS2 = 77 - jax.random.randint(jax.random.fold_in(_rk, 8), (2,), 0, max(1, 77 // 4) + 1, jnp.int32)
        _ctx_1024P = jax.random.normal(jax.random.fold_in(_rk, 11), (2, 16, 512), jnp.float32)
        _ctx_1024c = jax.random.dirichlet(jax.random.fold_in(_rk, 511), 0.3 * jnp.ones((16,), jnp.float32), (2, 77))
        _ctx_1024t = jnp.einsum('bsk,bkd->bsd', _ctx_1024c, _ctx_1024P)
        _ctx_1024t = _ctx_1024t * jax.lax.rsqrt(jnp.mean(jnp.square(_ctx_1024t)) + 1e-12) * 0.953939
        ctx_1024 = 2.81802e-05 + 1.00001 * (_ctx_1024t + 0.3 * jax.random.normal(jax.random.fold_in(_rk, 611), (2, 77, 512), jnp.float32))
        _validS = jnp.arange(2048)[None, :] < _lenS[:, None]
        _validS2 = jnp.arange(77)[None, :] < _lenS2[:, None]
        _causal = jnp.tril(jnp.ones((2048, 2048), dtype=bool))
        mask_BxSxS2_ik0 = jnp.where(jnp.broadcast_to(_validS2[:, None, :], (2, 2048, 77)), 0, 1).astype(jnp.int32)
        _g = jax.random.normal(jax.random.fold_in(_rk, 9001), (2, 1), jnp.float32)
        _g = jnp.sign(_g) * jnp.maximum(jnp.abs(_g), 1.0) + (_g == 0) * 1.0
        g_xattn = _g[0]
        g_ffn = _g[1]
        return (x, ctx_1024, mask_BxSxS2_ik0, g_xattn, g_ffn)
    x, ctx_1024, mask_BxSxS2_ik0, g_xattn, g_ffn = _rec_inputs()

    def _L0_xattn_setup():
        import jax, jax.numpy as jnp
        import numpy as np
        E = 512
        B, QL, KVL = (8, 1024, 1024)
        key = jax.random.key(seed)
        ks = jax.random.split(key, 12)
        s = 1.0 / np.sqrt(E)
        return {'query': jax.random.normal(ks[0], (B, QL, E), jnp.float32), 'key_value': jax.random.normal(ks[1], (B, KVL, E), jnp.float32), 'attention_mask': jax.random.randint(ks[2], (B, QL, KVL), 0, 2, jnp.int32), 'Wq': jax.random.uniform(ks[3], (E, E), jnp.float32, -s, s), 'bq': jax.random.uniform(ks[4], (E,), jnp.float32, -s, s), 'Wk': jax.random.uniform(ks[5], (E, E), jnp.float32, -s, s), 'bk': jax.random.uniform(ks[6], (E,), jnp.float32, -s, s), 'Wv': jax.random.uniform(ks[7], (E, E), jnp.float32, -s, s), 'bv': jax.random.uniform(ks[8], (E,), jnp.float32, -s, s), 'Wo': jax.random.uniform(ks[9], (E, E), jnp.float32, -s, s), 'bo': jax.random.uniform(ks[10], (E,), jnp.float32, -s, s)}
    _L0_xattn_all = _L0_xattn_setup()
    _L0_xattn_in = {k: v for k, v in _L0_xattn_all.items() if k in ('Wq', 'bq', 'Wk', 'bk', 'Wv', 'bv', 'Wo', 'bo')}
    del _L0_xattn_all

    def _L0_ffn_setup():
        import jax, jax.numpy as jnp
        import numpy as np
        NUM_EXPERTS = 8
        EXPERT_CAPACITY = 2.0
        DIM = 512
        HIDDEN_DIM = 2048
        key = jax.random.key(seed)
        k_x, k_g, k_w1, k_w2 = jax.random.split(key, 4)
        n, t, d, f, e = (8, 512, DIM, HIDDEN_DIM, NUM_EXPERTS)
        x = jax.random.normal(k_x, (n, t, d), dtype=jnp.float32)
        gate_w = jax.random.normal(k_g, (e, d), dtype=jnp.float32) * 0.02
        w1 = jax.random.normal(k_w1, (e, d, f), dtype=jnp.float32) * 0.02
        w2 = jax.random.normal(k_w2, (e, f, d), dtype=jnp.float32) * 0.02
        return {'x': x, 'gate_w': gate_w, 'w1': w1, 'w2': w2}
    _L0_ffn_all = _L0_ffn_setup()
    _L0_ffn_in = {k: v for k, v in _L0_ffn_all.items() if k in ('gate_w', 'w1', 'w2')}
    del _L0_ffn_all
    return {'x': x, 'ctx_1024': ctx_1024, 'mask_BxSxS2_ik0': mask_BxSxS2_ik0, 'g_xattn': g_xattn, 'g_ffn': g_ffn, 'L0_xattn_Wq': _L0_xattn_in['Wq'], 'L0_xattn_bq': _L0_xattn_in['bq'], 'L0_xattn_Wk': _L0_xattn_in['Wk'], 'L0_xattn_bk': _L0_xattn_in['bk'], 'L0_xattn_Wv': _L0_xattn_in['Wv'], 'L0_xattn_bv': _L0_xattn_in['bv'], 'L0_xattn_Wo': _L0_xattn_in['Wo'], 'L0_xattn_bo': _L0_xattn_in['bo'], 'L0_ffn_gate_w': _L0_ffn_in['gate_w'], 'L0_ffn_w1': _L0_ffn_in['w1'], 'L0_ffn_w2': _L0_ffn_in['w2']}

def reference(x, ctx_1024, mask_BxSxS2_ik0, g_xattn, g_ffn, L0_xattn_Wq, L0_xattn_bq, L0_xattn_Wk, L0_xattn_bk, L0_xattn_Wv, L0_xattn_bv, L0_xattn_Wo, L0_xattn_bo, L0_ffn_gate_w, L0_ffn_w1, L0_ffn_w2):
    import jax
    import jax.numpy as jnp

    def _L0_xattn_ref(query, key_value, attention_mask, Wq, bq, Wk, bk, Wv, bv, Wo, bo):
        import jax, jax.numpy as jnp
        import numpy as np
        E = 512
        B, QL, KVL = (8, 1024, 1024)
        q = jnp.einsum('bqe,fe->bqf', query, Wq) + bq
        k = jnp.einsum('bke,fe->bkf', key_value, Wk) + bk
        v = jnp.einsum('bke,fe->bkf', key_value, Wv) + bv
        scale = 1.0 / jnp.sqrt(jnp.asarray(q.shape[-1], q.dtype))
        attn = jnp.einsum('bqe,bke->bqk', q, k) * scale
        attn = jnp.where(attention_mask == 0, -jnp.inf, attn)
        attn = jax.nn.softmax(attn, axis=-1)
        out = jnp.einsum('bqk,bke->bqe', attn, v)
        out = jnp.einsum('bqe,fe->bqf', out, Wo) + bo
        return out

    def _L0_ffn_ref(x, gate_w, w1, w2):
        import jax, jax.numpy as jnp
        import numpy as np
        NUM_EXPERTS = 8
        EXPERT_CAPACITY = 2.0
        DIM = 512
        HIDDEN_DIM = 2048
        n, t, d = x.shape
        e = gate_w.shape[0]
        k = int(EXPERT_CAPACITY * t / e)
        scores = jnp.einsum('ntd,ed->nte', x, gate_w)
        probs = jax.nn.softmax(scores, axis=-1)
        g, m = jax.lax.top_k(probs.transpose(0, 2, 1), k)
        batch_idx = jnp.arange(n)[:, None, None]
        xin = x[batch_idx, m]
        h = jnp.einsum('nekd,edf->nekf', xin, w1)
        h = jax.nn.gelu(h, approximate=False)
        h = jnp.einsum('nekf,efd->nekd', h, w2)
        out_tok = g[..., None] * h
        out = jnp.zeros((n, t, d), dtype=x.dtype).at[batch_idx, m].add(out_tok)
        return out
    x = x + jnp.tanh(g_xattn[0]) * _L0_xattn_ref(_layernorm(x, axis=-1), ctx_1024, mask_BxSxS2_ik0, L0_xattn_Wq, L0_xattn_bq, L0_xattn_Wk, L0_xattn_bk, L0_xattn_Wv, L0_xattn_bv, L0_xattn_Wo, L0_xattn_bo)
    x = x + jnp.tanh(g_ffn[0]) * _L0_ffn_ref(_layernorm(x, axis=-1), L0_ffn_gate_w, L0_ffn_w1, L0_ffn_w2)
    return x

_drawn_inputs = setup_inputs


def setup_inputs(seed=0):
    import zlib

    import numpy as np

    out = dict(_drawn_inputs(seed))
    spreads = {}
    factors = {'L0_xattn_bq': 56.278, 'L0_xattn_bk': 64.0, 'L0_xattn_bv': 5.067, 'L0_xattn_bo': 2.794}
    for name, (base, spread) in spreads.items():
        noise = np.random.default_rng([zlib.crc32(name.encode()), seed]).standard_normal(out[name].shape)
        drawn = base * np.exp(spread * noise) if base else spread * noise
        out[name] = jnp.asarray(drawn.astype(out[name].dtype))
    for name, factor in factors.items():
        out[name] = (out[name] * factor).astype(out[name].dtype)
    return out
```

```python
from contextlib import ExitStack

import numpy as np

import concourse.bass as bass
from concourse import mybir

F32 = mybir.dt.float32
F32R = mybir.dt.float32r
BF16 = mybir.dt.bfloat16
I32 = mybir.dt.int32
U32 = mybir.dt.uint32
ALU = mybir.AluOpType
ACT = mybir.ActivationFunctionType
AX = mybir.AxisListType

P = 128
BANK = 512
EPS = 1e-5
MASKED = -1.0e30
TOP_BIT = 29


def wait(eng, sem, value):
    if not isinstance(value, int) or value > 0:
        eng.wait_ge(sem, value)


class Tally:

    def __init__(self, sem):
        self.sem, self.n = sem, 0

    def mark(self, ins):
        ins.then_inc(self.sem, 1)
        self.n += 1
        return self.n


def flamingo_layer(nc, x, ctx_in, mask, g_xattn, g_ffn, Wq, bq, Wk, bk, Wv, bv, Wo, bo, gate_w, w1, w2, out):
    B, S, D = x.shape
    J = ctx_in.shape[1]
    E, _, F = w1.shape
    CAP = 2 * S // E
    KD = D // P
    KF = F // P
    TB = S // P
    NT = B * TB
    Q = 4
    NQ = NT // Q
    QB = NQ // B
    NC = CAP // P
    G = B * E
    BJ = B * J
    NE = NT * E
    NV = 5
    SCALE = float(D) ** -0.5
    assert D == BANK and CAP == BANK and J <= P and KD == NC == 4 and KF == 16 and B == 2 and E == 8

    x_q = x.rearrange("b (q i p) d -> (b q) p i d", i=Q, p=P)
    out_rows = out.rearrange("b s d -> (b s) d")
    out_q = out_rows.rearrange("(q i p) d -> q p i d", i=Q, p=P)
    xn_rows = nc.dram_tensor("xn_rows", [B * S, D], F32, kind="Internal").ap()
    xn_q = xn_rows.rearrange("(q i p) d -> q p i d", i=Q, p=P)
    mask_v = mask.rearrange("b (t p) j -> p (b t) j", p=P)
    w1_v = w1.rearrange("e (k p) f -> e p k f", p=P)
    w2_v = w2.rearrange("e (c p) d -> e p c d", p=P)

    whole = ExitStack()
    with whole:
        def sem(name):
            return whole.enter_context(nc.semaphore(name))

        def keep(name, shape, dt):
            return whole.enter_context(nc.sbuf_tensor(name, shape, dt))

        bank = [whole.enter_context(nc.psum_tensor(f"bank{i}", [P, BANK], F32)) for i in range(8)]

        ident = keep("ident", [P, P], F32)
        iota_slot = keep("iota_slot", [P, P], BF16)
        iota_block = keep("iota_block", [P, NC], BF16)
        slot_lo = keep("slot_lo", [P, B, TB, E], BF16)
        slot_hi = keep("slot_hi", [P, B, TB, E], BF16)
        values = keep("values", [P, B, TB, E, NV], BF16)
        gates = keep("gates", [P, 2], F32)
        logits = keep("logits", [P, B, TB, E], F32)

        early = ExitStack()

        def first(name, shape, dt):
            return early.enter_context(nc.sbuf_tensor(name, shape, dt))

        with early:
            gates_raw = first("gates_raw", [P, 2], F32)
            ones_row = first("ones_row", [1, P], F32)
            bias_rows = first("bias_rows", [3 * KD, P], F32)
            bo_row = first("bo_row", [1, D], F32)
            gate_raw = first("gate_raw", [E, D], F32)
            cols = first("cols", [P, 3 * KD + KD * E], F32)
            ctx_raw = first("ctx_raw", [J, B, D], F32)
            raw_q = first("raw_q", [P, KD, D], F32)
            woT = first("woT", [P, KD, D], F32)
            ctxT = first("ctxT", [P, KD, B, J], F32)
            kT = first("kT", [P, KD, BJ], F32)
            vT = first("vT", [P, KD, BJ], F32)
            qk = first("qk", [P, KD, BJ], F32)
            qk_row = first("qk_row", [1, BJ], F32)
            vo = first("vo", [J, B, D], F32)
            mask_i = first("mask_i", [P, NT, J], I32)
            x_s = first("x_s", [P, 3, Q, D], F32)
            xn1 = first("xn1", [P, 2, Q, D], F32)
            xT = first("xT", [P, 2, Q, KD, P], F32)
            mbias = first("mbias", [P, 2, Q, J], F32)
            sc = first("sc", [P, 2, Q, J], F32)
            ex = first("ex", [P, 2, Q, J], F32)
            eT = first("eT", [J, 2, Q * P], F32)
            st1 = first("st1", [P, Q, 6], F32)
            st2 = first("st2", [P, Q, 6], F32)
            mv1 = first("mv1", [P, 2, Q, 2], F32)
            mv2 = first("mv2", [P, 2, Q, 2], F32)
            norm1 = first("norm1", [P, 2, 4, Q], F32)
            norm2 = first("norm2", [P, 2, 4, Q], F32)
            powers = first("powers", [P, Q], F32)
            smax = first("smax", [P, 2, Q], F32)
            smaxn = first("smaxn", [P, 2, Q], F32)
            rsum = first("rsum", [P, 2, Q], F32)
            rinv = first("rinv", [P, 2, Q], F32)
            with ExitStack() as raw:
                raw_k, raw_v, raw_o, wkT, wvT = (
                    raw.enter_context(nc.sbuf_tensor(n, [P, KD, D], F32))
                    for n in ("raw_k", "raw_v", "raw_o", "wkT", "wvT"))
            x1 = first("x1", [P, 2, Q, D], F32)
            xn2 = first("xn2", [P, 2, Q, D], F32)
            x2T = first("x2T", [P, 2, Q, KD, P], F32)

        w1h = keep("w1h", [P, KF, KD, P], F32R)
        w1l = keep("w1l", [P, KF, KD, P], F32R)
        w2h = keep("w2h", [P, KF, D], F32R)
        w2l = keep("w2l", [P, KF, D], F32R)
        raw1 = keep("raw1", [P, 2, KD, P], F32)
        raw2 = keep("raw2", [P, 2, D], F32)

        late = ExitStack()

        def choice(name, dt, shape=(P, B, TB, E)):
            return late.enter_context(nc.sbuf_tensor(name, list(shape), dt))

        with late:
            prob = choice("prob", F32)
            pexp = choice("pexp", F32)
            pstat = choice("pstat", F32, [P, 3, B, TB])
            ones_m = choice("ones_m", BF16, [P, P])
            below_m = choice("below_m", BF16, [P, P])
            thr = choice("thr", I32, [P, B, E])
            bit = choice("bit", I32, [P, B, E])
            cand = choice("cand", I32, [P, B, E])
            hit = choice("hit", F32, [P, B, E])
            atleast = choice("atleast", BF16)
            count = choice("count", BF16, [P, B, E])
            above = choice("above", BF16)
            tied = choice("tied", BF16)
            need = choice("need", F32, [P, B, E])
            chosen = choice("chosen", BF16)
            fits = choice("fits", BF16)
            place_i = choice("place_i", I32)
            part_i = choice("part_i", I32)
            gated = choice("gated", F32)
            rest = choice("rest", F32)
            vrow_i = choice("vrow_i", I32, [P, B, TB])
            vpar_i = choice("vpar_i", I32, [P, 1])
            iota_i = choice("iota_i", I32, [P, P])

        xTh = keep("xTh", [P, B, KD, CAP], F32R)
        xTl = keep("xTl", [P, B, KD, CAP], F32R)
        hf = keep("hf", [P, 2, CAP], F32)
        hh = keep("hh", [P, 2, CAP], F32R)
        hl = keep("hl", [P, 2, CAP], F32R)
        xg = keep("xg", [P, 2, D], F32)
        y = keep("y", [P, NC, D], F32)
        onehot = keep("onehot", [P, TB, P], BF16)
        blockhot = keep("blockhot", [P, TB, NC], BF16)
        carried = keep("carried", [P, TB, NC, NV], BF16)
        got = keep("got", [P, NC, NV], F32)
        slot_gate = keep("slot_gate", [P, B, 2, NC], F32)
        slot_row = keep("slot_row", [P, B, NC], U32)

        consts = sem("consts")
        pool_start = sem("pool_start")
        lin = [sem(f"lin{i}") for i in range(7)]
        prep_full = sem("prep_full")
        prep_act = sem("prep_act")
        prep_dve = sem("prep_dve")
        gates_done = sem("gates_done")
        x_in = [sem(f"x_in{i}") for i in range(3)]
        mask_in = sem("mask_in")
        stats1 = sem("stats1")
        stats2 = sem("stats2")
        pool_own = sem("pool_own")
        dve_own = sem("dve_own")
        normed1 = sem("normed1")
        normed2 = sem("normed2")
        turned = sem("turned")
        turn_out = sem("turn_out")
        scored = sem("scored")
        mask_ready = sem("mask_ready")
        sc_ready = sem("sc_ready")
        smax_ready = sem("smax_ready")
        exped = sem("exped")
        e_turned = sem("e_turned")
        e_out = sem("e_out")
        weighed = sem("weighed")
        added = sem("added")
        x1_out = [sem(f"x1_out{i}") for i in range(2)]
        xn_out = [sem(f"xn_out{i}") for i in range(2)]
        routed = sem("routed")
        logit_out = sem("logit_out")

        pdiff = sem("pdiff")
        pexped = sem("pexped")
        bit_count = sem("bit_count")
        bit_total = sem("bit_total")
        pick_in = sem("pick_in")
        pick_sum = sem("pick_sum")
        chosen_all = sem("chosen_all")

        w1_in = [sem(f"w1_in{i}") for i in range(2)]
        w2_in = [sem(f"w2_in{i}") for i in range(2)]
        w1_high = sem("w1_high")
        w2_high = sem("w2_high")
        w1_low = sem("w1_low")
        w2_low = sem("w2_low")
        hot = sem("hot")
        slots_sum = sem("slots_sum")
        slots_got = sem("slots_got")
        slots_own = sem("slots_own")
        slots_ready = sem("slots_ready")
        gathered = [sem(f"gathered{i}") for i in range(2)]
        gathers = sem("gathers")
        scatters = sem("scatters")
        x_turned = sem("x_turned")
        x_high = sem("x_high")
        x_split = sem("x_split")
        h_sum = sem("h_sum")
        h_act = sem("h_act")
        h_high = sem("h_high")
        h_split = sem("h_split")
        y_sum = sem("y_sum")
        y_act = sem("y_act")
        y_dve = sem("y_dve")
        scattered = [sem(f"scattered{i}") for i in range(NC)]

        block = whole.enter_context(nc.Block())

        steps = [("cols", 0, None)]
        steps += [("ctx", b, None) for b in range(B)]
        steps += [("turn_k", k, None) for k in range(KD)]
        steps += [("kT", h, 6) for h in range(2)]
        steps += [("qk_row", 0, 8)]
        steps += [("qk", h, 8) for h in range(2)]
        steps += [("turn_v", k, None) for k in range(KD)]
        steps += [("vT", h, 15) for h in range(2)]
        steps += [("turn_o", k, None) for k in range(KD)]
        steps += [("vo", b, 21) for b in range(B)]
        BC = 3 * KD
        needs_in = {"cols": (0, 5 * 16), "ctx": (1, 16), "turn_k": (2, 16), "qk": (3, 16), "turn_v": (4, 16),
                    "turn_o": (5, 16)}

        def wait_evacuated(eng, n):
            eng.wait_ge(prep_act, n // 2 + 1)
            if n >= 1:
                eng.wait_ge(prep_dve, (n + 1) // 2)

        def prep_pe(pe):
            pe.wait_ge(consts, 2)
            for n, (name, i, after) in enumerate(steps):
                bk = bank[n % 2]
                if name in needs_in:
                    which, value = needs_in[name]
                    pe.wait_ge(lin[which], value)
                if n >= 2:
                    pe.wait_ge(prep_act if n % 2 == 0 else prep_dve, n // 2)
                if after is not None:
                    wait_evacuated(pe, after)
                if name == "cols":
                    pe.transpose(bk[:, 0:BC], bias_rows[:, :], ident[0:BC, 0:BC])
                    for k in range(KD):
                        last = pe.transpose(bk[:, BC + k * E:BC + (k + 1) * E], gate_raw[:, k * P:(k + 1) * P],
                                            ident[0:E, 0:E])
                elif name == "ctx":
                    for k in range(KD):
                        last = pe.transpose(bk[:, k * J:(k + 1) * J], ctx_raw[:, i, k * P:(k + 1) * P],
                                            ident[0:J, 0:J])
                elif name.startswith("turn"):
                    raw_w = {"turn_k": raw_k, "turn_v": raw_v, "turn_o": raw_o}[name]
                    for c in range(KD):
                        last = pe.transpose(bk[:, c * P:(c + 1) * P], raw_w[:, c, i * P:(i + 1) * P], ident[:, :])
                elif name in ("kT", "vT"):
                    wt = wkT if name == "kT" else wvT
                    for h in range(2):
                        for k in range(KD):
                            c = 2 * i + h
                            last = pe.matmul(bk[:, h * BJ:(h + 1) * BJ], wt[:, k, c * P:(c + 1) * P],
                                             ctxT[:, k, :, :].rearrange("p b j -> p (b j)"),
                                             start=(k == 0), stop=(k == KD - 1))
                elif name == "qk_row":
                    for c in range(KD):
                        last = pe.matmul(bk[0:1, 0:BJ], cols[:, 2 * KD + c:2 * KD + c + 1], kT[:, c, :],
                                         start=(c == 0), stop=(c == KD - 1))
                elif name == "qk":
                    for h in range(2):
                        for c in range(KD):
                            d = 2 * i + h
                            last = pe.matmul(bk[:, h * BJ:(h + 1) * BJ], raw_q[:, c, d * P:(d + 1) * P], kT[:, c, :],
                                             start=(c == 0), stop=(c == KD - 1))
                elif name == "vo":
                    for c in range(KD):
                        pe.matmul(bk[0:J, :], vT[:, c, i * J:(i + 1) * J], woT[:, c, :], start=(c == 0), stop=False)
                    last = pe.matmul(bk[0:J, :], ones_row[:, 0:J], bo_row[:, :], start=False, stop=True)
                last.then_inc(prep_full, 1)

        def prep_out(eng, mine, is_act):
            def copy(dst, src, scale=None, bias=None):
                if is_act:
                    if bias is not None:
                        return eng.activation(dst, src, ACT.Identity, bias=bias)
                    return eng.activation(dst, src, ACT.Copy, scale=1.0 if scale is None else scale)
                if bias is not None:
                    return eng.tensor_scalar(dst, src, bias, None, ALU.add)
                if scale is not None:
                    return eng.tensor_scalar(dst, src, scale, None, ALU.mult)
                return eng.tensor_copy(dst, src)

            for n, (name, i, _) in enumerate(steps):
                if (n % 2 == 0) != is_act:
                    continue
                bk = bank[n % 2]
                eng.wait_ge(prep_full, n + 1)
                if name == "cols":
                    last = copy(cols[:, :], bk[:, 0:BC + KD * E])
                elif name == "ctx":
                    last = copy(ctxT[:, :, i, :], bk[:, 0:KD * J].rearrange("p (k j) -> p k j", k=KD))
                elif name == "turn_k":
                    last = copy(wkT[:, i, :], bk[:, :])
                elif name == "turn_v":
                    last = copy(wvT[:, i, :], bk[:, :])
                elif name == "turn_o":
                    last = copy(woT[:, i, :], bk[:, :])
                elif name in ("kT", "vT"):
                    eng.wait_ge(prep_act, 1)
                    for h in range(2):
                        c = 2 * i + h
                        at = c + (0 if name == "kT" else KD)
                        last = copy((kT if name == "kT" else vT)[:, c, :], bk[:, h * BJ:(h + 1) * BJ],
                                    bias=cols[:, at:at + 1])
                elif name == "qk_row":
                    last = copy(qk_row[:, :], bk[0:1, 0:BJ], scale=SCALE)
                elif name == "qk":
                    last = copy(qk[:, 2 * i:2 * i + 2, :], bk[:, 0:2 * BJ].rearrange("p (h j) -> p h j", h=2),
                                scale=SCALE)
                elif name == "vo":
                    eng.wait_ge(gates_done, 1)
                    last = copy(vo[:, i, :], bk[0:J, :], scale=gates[0:J, 0:1])
                last.then_inc(mine, 1)

        turns = []
        for it in range(NQ + 3):
            turns += [(1, it - 1, i) for i in range(Q) if 0 <= it - 1 < NQ]
            turns += [(2, it - 3, i) for i in range(Q) if 0 <= it - 3 < NQ]
        turn_at = {t: n for n, t in enumerate(turns)}
        T_BANKS = (2, 3, 4)
        SC_BANK, E_BANK, R_BANK = bank[5], bank[6], bank[7]
        O_BANKS = (bank[0], bank[1])

        def turn_pe(pe, which, q, i):
            n = turn_at[which, q, i]
            src = (xn1 if which == 1 else xn2)[:, q % 2, i, :]
            pe.wait_ge(normed1 if which == 1 else normed2, Q * q + i + 1)
            if n >= 3:
                pe.wait_ge(turn_out, n - 2)
            for k in range(KD):
                last = pe.transpose(bank[T_BANKS[n % 3]][:, k * P:(k + 1) * P], src[:, k * P:(k + 1) * P], ident[:, :])
            last.then_inc(turned, 1)

        def turn_act(act, which, q, i):
            n = turn_at[which, q, i]
            dst = (xT if which == 1 else x2T)[:, q % 2, i, :, :].rearrange("p k t -> p (k t)")
            act.wait_ge(turned, n + 1)
            if q >= 2:
                act.wait_ge(scored if which == 1 else routed, q - 1)
            act.activation(dst, bank[T_BANKS[n % 3]][:, :], ACT.Copy).then_inc(turn_out, 1)

        def attention_pe(pe):
            for it in range(NQ + 3):
                q = it - 1
                if 0 <= q < NQ:
                    for i in range(Q):
                        turn_pe(pe, 1, q, i)
                    if q == 0:
                        wait_evacuated(pe, len(steps) - 1)
                    if q >= 1:
                        pe.wait_ge(sc_ready, q)
                    b = q // QB
                    for i in range(Q):
                        pe.wait_ge(turn_out, turn_at[1, q, i] + 1)
                        for k in range(KD):
                            pe.matmul(SC_BANK[:, i * J:(i + 1) * J], xT[:, q % 2, i, k, :],
                                      qk[:, k, b * J:(b + 1) * J], start=(k == 0), stop=False)
                        last = pe.matmul(SC_BANK[:, i * J:(i + 1) * J], ones_row[:, :], qk_row[:, b * J:(b + 1) * J],
                                         start=False, stop=True)
                    last.then_inc(scored, 1)
                q = it - 2
                if 0 <= q < NQ:
                    pe.wait_ge(exped, q + 1)
                    if q >= 1:
                        pe.wait_ge(e_out, q)
                    for i in range(Q):
                        last = pe.transpose(E_BANK[0:J, i * P:(i + 1) * P], ex[:, q % 2, i, :], ident[:, :])
                    last.then_inc(e_turned, 1)
                    pe.wait_ge(e_out, q + 1)
                    for i in range(Q):
                        n = Q * q + i
                        if n >= 2:
                            pe.wait_ge(added, n - 1)
                        pe.matmul(O_BANKS[n % 2][:, :], eT[:, q % 2, i * P:(i + 1) * P], vo[:, q // QB, :],
                                  start=True, stop=True).then_inc(weighed, 1)
                q = it - 3
                if 0 <= q < NQ:
                    for i in range(Q):
                        turn_pe(pe, 2, q, i)
                    if q >= 1:
                        pe.wait_ge(logit_out, q)
                    for i in range(Q):
                        pe.wait_ge(turn_out, turn_at[2, q, i] + 1)
                        for k in range(KD):
                            last = pe.matmul(R_BANK[:, i * E:(i + 1) * E], x2T[:, q % 2, i, k, :],
                                             cols[:, BC + k * E:BC + (k + 1) * E], start=(k == 0), stop=(k == KD - 1))
                    last.then_inc(routed, 1)

        def attention_act(act):
            for it in range(NQ + 3):
                if 0 <= it - 1 < NQ:
                    for i in range(Q):
                        turn_act(act, 1, it - 1, i)
                q = it - 2
                if 0 <= q < NQ:
                    act.wait_ge(e_turned, q + 1)
                    if q >= 2:
                        act.wait_ge(weighed, Q * (q - 1))
                    act.activation(eT[:, q % 2, :], E_BANK[0:J, :], ACT.Copy).then_inc(e_out, 1)
                if 0 <= it - 3 < NQ:
                    for i in range(Q):
                        turn_act(act, 2, it - 3, i)
                q = it - 1
                if 0 <= q < NQ:
                    act.wait_ge(smax_ready, q + 1)
                    if q >= 2:
                        act.wait_ge(e_turned, q - 1)
                        act.wait_ge(added, Q * (q - 1))
                    for i in range(Q):
                        last = act.activation(ex[:, q % 2, i, :], sc[:, q % 2, i, :], ACT.Exp,
                                              bias=smaxn[:, q % 2, i:i + 1], accum_out=rsum[:, q % 2, i:i + 1])
                    last.then_inc(exped, 1)

        def attention_pool(pool):
            own = Tally(pool_own)

            def norm(mv, nm, src, dst, done, q):
                s = q % 2
                own.mark(pool.tensor_scalar(nm[:, s, 0, :], mv[:, s, :, 1], EPS, None, ALU.add))
                own.mark(pool.tensor_scalar(nm[:, s, 1, :], mv[:, s, :, 0], -1.0, None, ALU.mult))
                pool.wait_ge(pool_own, own.n)
                own.mark(pool.tensor_tensor(nm[:, s, 2, :], nm[:, s, 0, :], powers[:, :], ALU.pow))
                pool.wait_ge(pool_own, own.n)
                own.mark(pool.tensor_tensor(nm[:, s, 3, :], nm[:, s, 1, :], nm[:, s, 2, :], ALU.mult))
                pool.wait_ge(pool_own, own.n)
                for i in range(Q):
                    pool.tensor_scalar(dst[:, s, i, :], src[:, i, :], nm[:, s, 2, i:i + 1], nm[:, s, 3, i:i + 1],
                                       ALU.mult, ALU.add).then_inc(done, 1)

            for it in range(NQ + 2):
                q = it
                if q < NQ:
                    pool.wait_ge(stats1, q + 1)
                    if q >= 2:
                        pool.wait_ge(turned, turn_at[1, q - 2, Q - 1] + 1)
                    norm(mv1, norm1, x_s[:, q % 3, :, :], xn1, normed1, q)
                q = it - 1
                if 0 <= q < NQ:
                    if q == 0:
                        pool.wait_ge(mask_in, 16)
                    if q >= 2:
                        pool.wait_ge(sc_ready, q - 1)
                    pool.tensor_scalar(mbias[:, q % 2, :, :], mask_i[:, Q * q:Q * q + Q, :], 0.0, MASKED,
                                       ALU.is_equal, ALU.mult).then_inc(mask_ready, 1)
                q = it - 2
                if 0 <= q < NQ:
                    pool.wait_ge(stats2, q + 1)
                    if q >= 2:
                        pool.wait_ge(turned, turn_at[2, q - 2, Q - 1] + 1)
                        pool.wait_ge(xn_out[q % 2], 16 * (q // 2))
                    norm(mv2, norm2, x1[:, q % 2, :, :], xn2, normed2, q)

        def attention_dve(dve):
            own = Tally(dve_own)

            def stats(src, st, mv, done, q):
                for i in range(Q):
                    own.mark(dve.bn_stats(st[:, i, :], src[:, i, :]))
                dve.wait_ge(dve_own, own.n)
                for i in range(Q):
                    last = dve.bn_aggr(mv[:, q % 2, i, :], st[:, i, :])
                    own.mark(last) if i < Q - 1 else last.then_inc(done, 1)

            for it in range(NQ + 3):
                q = it
                if q < NQ:
                    dve.wait_ge(x_in[q % 3], 16 * (q // 3 + 1))
                    if q >= 2:
                        dve.wait_ge(normed1, Q * (q - 1))
                    if q >= 1:
                        dve.wait_ge(stats1, q)
                    stats(x_s[:, q % 3, :, :], st1, mv1, stats1, q)
                q = it - 2
                if 0 <= q < NQ:
                    dve.wait_ge(exped, q + 1)
                    own.mark(dve.reciprocal(rinv[:, q % 2, :], rsum[:, q % 2, :]))
                    dve.wait_ge(dve_own, own.n)
                    if q >= 2:
                        dve.wait_ge(x1_out[q % 2], 16 * (q // 2))
                        dve.wait_ge(normed2, Q * (q - 1))
                    for i in range(Q):
                        n = Q * q + i
                        dve.wait_ge(weighed, n + 1)
                        dve.scalar_tensor_tensor(out=x1[:, q % 2, i, :], in0=O_BANKS[n % 2][:, :],
                                                 scalar=rinv[:, q % 2, i:i + 1], in1=x_s[:, q % 3, i, :],
                                                 op0=ALU.mult, op1=ALU.add).then_inc(added, 1)
                    dve.wait_ge(added, Q * q + Q)
                    if q >= 1:
                        dve.wait_ge(stats2, q)
                    stats(x1[:, q % 2, :, :], st2, mv2, stats2, q)
                q = it - 1
                if 0 <= q < NQ:
                    dve.wait_ge(scored, q + 1)
                    dve.wait_ge(mask_ready, q + 1)
                    dve.tensor_tensor(sc[:, q % 2, :, :], SC_BANK[:, 0:Q * J].rearrange("p (i j) -> p i j", i=Q),
                                      mbias[:, q % 2, :, :], ALU.add).then_inc(sc_ready, 1)
                    dve.wait_ge(sc_ready, q + 1)
                    own.mark(dve.tensor_reduce(smax[:, q % 2, :], sc[:, q % 2, :, :], AX.X, ALU.max))
                    dve.wait_ge(dve_own, own.n)
                    dve.tensor_scalar(smaxn[:, q % 2, :], smax[:, q % 2, :], -1.0, None, ALU.mult)\
                       .then_inc(smax_ready, 1)
                q = it - 3
                if 0 <= q < NQ:
                    dve.wait_ge(routed, q + 1)
                    dve.tensor_copy(logits[:, q // QB, (q % QB) * Q:(q % QB) * Q + Q, :],
                                    R_BANK[:, 0:Q * E].rearrange("p (i e) -> p i e", i=Q)).then_inc(logit_out, 1)

        def rows_stored(eng):
            for i in range(2):
                eng.wait_ge(x1_out[i], 16 * (NQ // 2))
                eng.wait_ge(xn_out[i], 16 * (NQ // 2))

        COUNT_BANK, PICK_BANK, PLACE_BANK, NEED_BANK = bank[0], bank[1], bank[2], bank[3]

        def flat(t):
            return t[:, :, :, :].rearrange("p b t e -> p (b t) e")

        def over_tiles(t):
            return t.unsqueeze(2).to_broadcast([P, B, TB, E])

        candf, thrf = cand[:, :, :].bitcast(F32), thr[:, :, :].bitcast(F32)

        def tile_counts(dve, flags):
            with nc.allow_low_precision(reason="counts up to 16"):
                return dve.tensor_reduce(count[:, :, :], flags[:, :, :, :].rearrange("p b t e -> p b e t"), AX.X,
                                         ALU.add)

        def choice_dve(dve, base):
            own = Tally(dve_own)
            own.n = base

            def step(ins):
                own.mark(ins)
                dve.wait_ge(dve_own, own.n)

            dve.wait_ge(logit_out, NQ)
            rows_stored(dve)
            lg, pr, pe_ = flat(logits), flat(prob), flat(pexp)

            def stat(i):
                return pstat[:, i, :, :].rearrange("p b t -> p (b t)")

            def over_e(i):
                return stat(i).unsqueeze(2).to_broadcast([P, NT, E])

            step(dve.tensor_reduce(stat(0), lg, AX.X, ALU.max))
            dve.tensor_tensor(pr, lg, over_e(0), ALU.subtract).then_inc(pdiff, 1)
            dve.memset(thr[:, :, :], 0)
            own.mark(dve.memset(bit[:, :, :], 1 << TOP_BIT))
            dve.wait_ge(pexped, 1)
            step(dve.tensor_reduce(stat(1), pe_, AX.X, ALU.add))
            step(dve.reciprocal(stat(2), stat(1)))
            step(dve.tensor_tensor(pr, pe_, over_e(2), ALU.mult))
            start = own.n
            per = 5
            with dve.Fori(0, TOP_BIT + 1) as r:
                dve.tensor_tensor(cand[:, :, :], thr[:, :, :], bit[:, :, :], ALU.bitwise_or).then_inc(dve_own, 1)
                dve.wait_ge(dve_own, r * per + start + 1)
                dve.tensor_tensor(atleast[:, :, :, :], prob[:, :, :, :], over_tiles(candf),
                                  ALU.is_ge).then_inc(dve_own, 1)
                dve.wait_ge(dve_own, r * per + start + 2)
                tile_counts(dve, atleast).then_inc(bit_count, 1)
                dve.tensor_scalar(bit[:, :, :], bit[:, :, :], 1, None, ALU.logical_shift_right).then_inc(dve_own, 1)
                dve.wait_ge(bit_total, r + 1)
                dve.scalar_tensor_tensor(out=hit[:, :, :], in0=COUNT_BANK[:, 0:G].rearrange("p (b e) -> p b e", b=B),
                                         scalar=float(CAP), in1=candf, op0=ALU.is_ge, op1=ALU.mult)\
                   .then_inc(dve_own, 1)
                dve.wait_ge(dve_own, r * per + start + 4)
                dve.tensor_tensor(thrf, thrf, hit[:, :, :], ALU.max).then_inc(dve_own, 1)
                dve.wait_ge(dve_own, r * per + start + 5)
            own.n = start + per * (TOP_BIT + 1)
            step(dve.tensor_tensor(above[:, :, :, :], prob[:, :, :, :], over_tiles(thrf), ALU.is_gt))
            step(dve.tensor_tensor(tied[:, :, :, :], prob[:, :, :, :], over_tiles(thrf), ALU.is_equal))
            tile_counts(dve, above).then_inc(pick_in, 1)
            dve.wait_ge(gates_done, 1)
            step(dve.tensor_scalar(flat(gated), pr, gates[:, 1:2], None, ALU.mult))
            vals = values[:, :, :, :, :].rearrange("p b t e v -> p (b t) e v")
            step(dve.tensor_copy(vals[:, :, :, 2], flat(gated)))
            step(dve.tensor_tensor(flat(rest), flat(gated), vals[:, :, :, 2], ALU.subtract))
            step(dve.tensor_copy(vals[:, :, :, 3], flat(rest)))
            step(dve.tensor_tensor(flat(gated), flat(rest), vals[:, :, :, 3], ALU.subtract))
            step(dve.tensor_copy(vals[:, :, :, 4], flat(gated)))
            dve.wait_ge(consts, CONSTS)
            step(dve.tensor_copy(vals[:, :, :, 0], vrow_i[:, :, :].rearrange("p b t -> p (b t)").unsqueeze(2)
                                 .to_broadcast([P, NT, E])))
            step(dve.tensor_copy(vals[:, :, :, 1], vpar_i[:, 0:1].unsqueeze(2).to_broadcast([P, NT, E])))
            step(dve.tensor_copy(iota_slot[:, :], iota_i[:, :]))
            step(dve.tensor_scalar(iota_block[:, :], iota_i[:, 0:NC], 1.0, None, ALU.add))
            dve.wait_ge(pick_sum, 1)
            step(dve.tensor_scalar(need[:, :, :], NEED_BANK[:, 0:G].rearrange("p (b e) -> p b e", b=B), -1.0,
                                   float(CAP), ALU.mult, ALU.add))
            step(dve.tensor_tensor(fits[:, :, :, :], PICK_BANK[:, 0:NE].rearrange("p (b t e) -> p b t e", b=B, t=TB),
                                   over_tiles(need[:, :, :]), ALU.is_lt))
            step(dve.tensor_tensor(fits[:, :, :, :], fits[:, :, :, :], tied[:, :, :, :], ALU.mult))
            dve.tensor_tensor(chosen[:, :, :, :], above[:, :, :, :], fits[:, :, :, :], ALU.add).then_inc(pick_in, 1)
            dve.wait_ge(pick_sum, 2)
            step(dve.tensor_copy(flat(place_i), PLACE_BANK[:, 0:NE].rearrange("p (n e) -> p n e", e=E)))
            step(dve.tensor_scalar(flat(part_i), flat(place_i), P - 1, None, ALU.bitwise_and))
            step(dve.tensor_copy(flat(slot_lo), flat(part_i)))
            step(dve.tensor_scalar(flat(part_i), flat(place_i), 7, None, ALU.logical_shift_right))
            dve.wait_ge(pick_in, 2)
            dve.scalar_tensor_tensor(out=flat(slot_hi), in0=flat(part_i), scalar=1.0, in1=flat(chosen),
                                     op0=ALU.add, op1=ALU.mult).then_inc(chosen_all, 1)
            dve.wait_ge(chosen_all, 1)

        def running_place(pe, dst, flags):
            d = dst[:, 0:NE].rearrange("p (b t e) -> p b (t e)", b=B, t=TB)
            f = flags[:, :, :, :].rearrange("p b t e -> p b (t e)")
            for s in range(1, TB):
                pe.matmul(d[:, :, s * E:], ones_m[:, :], f[:, :, 0:(TB - s) * E], start=(s == 1), stop=False,
                          skip_group_check=True)
            return pe.matmul(d, below_m[:, :], f, start=False, stop=True, skip_group_check=True)

        def choice_pe(pe):
            pe.wait_ge(consts, CONSTS)
            with pe.Fori(0, TOP_BIT + 1) as r:
                pe.wait_ge(bit_count, r + 1)
                pe.matmul(COUNT_BANK[:, 0:G], ones_m[:, :], count[:, :, :].rearrange("p b e -> p (b e)"),
                          start=True, stop=True).then_inc(bit_total, 1)
            pe.wait_ge(pick_in, 1)
            pe.matmul(NEED_BANK[:, 0:G], ones_m[:, :], count[:, :, :].rearrange("p b e -> p (b e)"),
                      start=True, stop=True)
            running_place(pe, PICK_BANK, tied).then_inc(pick_sum, 1)
            pe.wait_ge(pick_in, 2)
            running_place(pe, PLACE_BANK, chosen).then_inc(pick_sum, 1)

        H_BANKS = (bank[4], bank[5])
        Y_BANKS = (bank[0], bank[1], bank[2], bank[3])
        X_BANK, SLOT_BANK = bank[6], bank[7]
        LAG = 2

        def hidden_pe(pe, e, b, f, first_of_all=False):
            n = e * 2 * KF + b * KF + f
            if f == 0:
                pe.wait_ge(x_split, (e * 2 + b + 1) * NC)
            if b == 0:
                pe.wait_ge(w1_low, e * KF + f + 1)
            wait(pe, h_act, n - 1)
            for k in range(KD):
                for wpart, xpart in ((w1h, xTh), (w1h, xTl), (w1l, xTh)):
                    last = pe.matmul(H_BANKS[f % 2][:, :], wpart[:, f, k, :], xpart[:, b, k, :],
                                     start=(k == 0 and wpart is w1h and xpart is xTh),
                                     stop=(k == KD - 1 and wpart is w1l))
            last.then_inc(h_sum, 1)

        def output_pe(pe, e, b, f):
            n = e * 2 * KF + b * KF + f
            pe.wait_ge(h_split, n + 1)
            if b == 0:
                pe.wait_ge(w2_low, e * KF + f + 1)
            if f == 0:
                wait(pe, y_act, (e * 2 + b) * 2)
                wait(pe, y_dve, (e * 2 + b) * 2)
            for c in range(NC):
                for hpart, wpart in ((hh, w2h), (hh, w2l), (hl, w2h)):
                    last = pe.matmul(Y_BANKS[c][:, :], hpart[:, f % 2, c * P:(c + 1) * P], wpart[:, f, :],
                                     start=(f == 0 and hpart is hh and wpart is w2h),
                                     stop=(f == KF - 1 and hpart is hl))
            last.then_inc(y_sum, 1)

        def slots_pe(pe, g):
            pe.wait_ge(hot, g + 1)
            for t in range(TB):
                last = pe.matmul(SLOT_BANK[:, 0:NC * NV], onehot[:, t, :],
                                 carried[:, t, :, :].rearrange("p c v -> p (c v)"),
                                 start=(t == 0), stop=(t == TB - 1))
            last.then_inc(slots_sum, 1)

        def tokens_pe(pe, g, c):
            pe.wait_ge(gathered[c % 2], (g * 2 + c // 2 + 1) * 16)
            wait(pe, x_split, g * NC + c)
            for k in range(KD):
                last = pe.transpose(X_BANK[:, k * P:(k + 1) * P], xg[:, c % 2, k * P:(k + 1) * P], ident[:, :])
            last.then_inc(x_turned, 1)

        def hot_dve(dve, g, e, b):
            wait(dve, slots_sum, g)
            lo = slot_lo[:, b, :, bass.ds(e, 1)] if not isinstance(e, int) else slot_lo[:, b, :, e:e + 1]
            hi = slot_hi[:, b, :, bass.ds(e, 1)] if not isinstance(e, int) else slot_hi[:, b, :, e:e + 1]
            va = values[:, b, :, bass.ds(e, 1), :] if not isinstance(e, int) else values[:, b, :, e:e + 1, :]
            dve.tensor_tensor(onehot[:, :, :], iota_slot[:, :].unsqueeze(1).to_broadcast([P, TB, P]),
                              lo.to_broadcast([P, TB, P]), ALU.is_equal)
            dve.tensor_tensor(blockhot[:, :, :], iota_block[:, :].unsqueeze(1).to_broadcast([P, TB, NC]),
                              hi.to_broadcast([P, TB, NC]), ALU.is_equal).then_inc(slots_own, 1)
            dve.wait_ge(slots_own, g * 4 + 1)
            dve.tensor_tensor(carried[:, :, :, :], blockhot[:, :, :].unsqueeze(3).to_broadcast([P, TB, NC, NV]),
                              va.to_broadcast([P, TB, NC, NV]), ALU.mult).then_inc(hot, 1)

        def slots_dve(dve, g, b):
            dve.wait_ge(slots_sum, g + 1)
            dve.tensor_copy(got[:, :, :], SLOT_BANK[:, 0:NC * NV].rearrange("p (c v) -> p c v", c=NC))\
               .then_inc(slots_own, 1)
            dve.wait_ge(slots_own, g * 4 + 2)
            dve.tensor_tensor(slot_gate[:, b, 0, :], got[:, :, 3], got[:, :, 4], ALU.add).then_inc(slots_own, 1)
            dve.wait_ge(slots_own, g * 4 + 3)
            dve.tensor_tensor(slot_gate[:, b, 1, :], got[:, :, 2], slot_gate[:, b, 0, :], ALU.add)\
               .then_inc(slots_own, 1)
            for c in range(NC):
                wait(dve, scattered[c], (g - 1) * 16)
            dve.scalar_tensor_tensor(out=slot_row[:, b, :], in0=got[:, :, 0], scalar=float(P), in1=got[:, :, 1],
                                     op0=ALU.mult, op1=ALU.add).then_inc(slots_ready, 1)

        def split_tokens_dve(dve, g, b, c):
            dve.wait_ge(x_turned, g * NC + c + 1)
            src = X_BANK[:, :].rearrange("p (k t) -> p k t", k=KD)
            high, low = xTh[:, b, :, c * P:(c + 1) * P], xTl[:, b, :, c * P:(c + 1) * P]
            dve.tensor_copy(high, src).then_inc(x_high, 1)
            dve.wait_ge(x_high, g * NC + c + 1)
            dve.tensor_tensor(low, src, high.bitcast(F32), ALU.subtract).then_inc(x_split, 1)

        def split_hidden_dve(dve, e, b, f):
            n = e * 2 * KF + b * KF + f
            dve.wait_ge(h_act, n + 1)
            wait(dve, y_sum, n - 1)
            dve.tensor_copy(hh[:, f % 2, :], hf[:, f % 2, :]).then_inc(h_high, 1)
            dve.wait_ge(h_high, n + 1)
            dve.tensor_tensor(hl[:, f % 2, :], hf[:, f % 2, :], hh[:, f % 2, :].bitcast(F32), ALU.subtract)\
               .then_inc(h_split, 1)

        def gelu_act(act, e, b, f):
            n = e * 2 * KF + b * KF + f
            act.wait_ge(h_sum, n + 1)
            wait(act, h_split, n - 1)
            act.activation(hf[:, f % 2, :], H_BANKS[f % 2][:, :], ACT.Gelu).then_inc(h_act, 1)

        def output_rows(eng, e, b, c, done):
            g = e * 2 + b
            eng.wait_ge(y_sum, e * 2 * KF + (b + 1) * KF)
            wait(eng, scattered[c], g * 16)
            gate = slot_gate[:, b, 1, c:c + 1]
            if eng is nc.scalar:
                ins = eng.activation(y[:, c, :], Y_BANKS[c][:, :], ACT.Copy, scale=gate)
            else:
                ins = eng.tensor_scalar(y[:, c, :], Y_BANKS[c][:, :], gate, None, ALU.mult)
            ins.then_inc(done, 1)

        def weight_high_act(act, e, f):
            n = e * KF + f
            used = (e - 1) * 2 * KF + KF + f + 1
            wait(act, h_sum, used)
            wait(act, y_sum, used)
            act.wait_ge(w1_in[f % 2], e * (KF // 2) * 16 + (f // 2 + 1) * 16)
            act.activation(w1h[:, f, :, :], raw1[:, f % 2, :, :], ACT.Copy).then_inc(w1_high, 1)
            act.wait_ge(w2_in[f % 2], e * (KF // 2) * 16 + (f // 2 + 1) * 16)
            act.activation(w2h[:, f, :], raw2[:, f % 2, :], ACT.Copy).then_inc(w2_high, 1)

        def weight_low_pool(pool, e, f):
            n = e * KF + f
            pool.wait_ge(w1_high, n + 1)
            pool.tensor_tensor(w1l[:, f, :, :], raw1[:, f % 2, :, :], w1h[:, f, :, :].bitcast(F32), ALU.subtract)\
                .then_inc(w1_low, 1)
            pool.wait_ge(w2_high, n + 1)
            pool.tensor_tensor(w2l[:, f, :], raw2[:, f % 2, :], w2h[:, f, :].bitcast(F32), ALU.subtract)\
                .then_inc(w2_low, 1)

        def gather_pool(pool, g, b, c):
            pool.wait_ge(slots_ready, g + 1)
            wait(pool, x_turned, g * NC + c - 1)
            pool.sem_inc(gathers, 1)
            pool.indirect_dma_start(xg[:, c % 2, :], None, xn_rows,
                                    bass.IndirectOffsetOnAxis(ap=slot_row[:, b, c:c + 1], axis=0))\
                .then_inc(gathered[c % 2], 16)

        def scatter_pool(pool, e, b, c):
            g = e * 2 + b
            done, at = (y_act, c) if c < 2 else (y_dve, c - 2)
            pool.wait_ge(done, g * 2 + at + 1)
            for other in range(NC):
                wait(pool, scattered[other], g * 16)
            pool.sem_inc(scatters, 1)
            pool.indirect_dma_start(out_rows, bass.IndirectOffsetOnAxis(ap=slot_row[:, b, c:c + 1], axis=0),
                                    y[:, c, :], None, compute_op=ALU.add).then_inc(scattered[c], 16)

        HOT, SLOTS, FIRST_TURN = 1, 3, 6

        def next_group(e, b):
            return (e, 1) if b == 0 else (e + 1, 0)

        def group(e, b, last, at_step, at_end):
            for f in range(KF):
                at_step(f)
            at_end()

        def expert_pe(pe, e, final):
            for b in range(B):
                end = final and b == B - 1
                ne, nb = next_group(e, b)
                g = e * 2 + b + 1
                for f in range(KF):
                    if f + 1 < KF:
                        hidden_pe(pe, e, b, f + 1)
                    elif not end:
                        hidden_pe(pe, ne, nb, 0)
                    if not end and f == SLOTS:
                        slots_pe(pe, g)
                    if not end and f >= FIRST_TURN and (f - FIRST_TURN) % 2 == 0 and (f - FIRST_TURN) // 2 < NC:
                        tokens_pe(pe, g, (f - FIRST_TURN) // 2)
                    output_pe(pe, e, b, f)

        def expert_dve(dve, e, final):
            for b in range(B):
                end = final and b == B - 1
                ne, nb = next_group(e, b)
                g = e * 2 + b + 1
                for f in range(KF):
                    if f + 1 < KF:
                        split_hidden_dve(dve, e, b, f + 1)
                    elif not end:
                        split_hidden_dve(dve, ne, nb, 0)
                    if end:
                        continue
                    if f == HOT:
                        hot_dve(dve, g, ne, nb)
                    if f == SLOTS:
                        slots_dve(dve, g, nb)
                    if f >= FIRST_TURN and (f - FIRST_TURN) % 2 == 0 and (f - FIRST_TURN) // 2 < NC:
                        split_tokens_dve(dve, g, nb, (f - FIRST_TURN) // 2)
                for c in (2, 3):
                    output_rows(dve, e, b, c, y_dve)

        def expert_act(act, e, final):
            for b in range(B):
                end = final and b == B - 1
                ne, nb = next_group(e, b)
                for f in range(KF):
                    if f + 1 < KF:
                        gelu_act(act, e, b, f + 1)
                    elif not end:
                        gelu_act(act, ne, nb, 0)
                    if b == 0 and f < LAG:
                        weight_high_act(act, e, KF - LAG + f)
                    if b == 1 and f >= LAG and not final:
                        weight_high_act(act, e + 1, f - LAG)
                for c in (0, 1):
                    output_rows(act, e, b, c, y_act)

        def expert_pool(pool, e, final):
            for b in range(B):
                end = final and b == B - 1
                ne, nb = next_group(e, b)
                g = e * 2 + b + 1
                for f in range(KF):
                    if b == 0 and f < LAG:
                        weight_low_pool(pool, e, KF - LAG + f)
                    if b == 1 and f >= LAG and not final:
                        weight_low_pool(pool, e + 1, f - LAG)
                    if not end and f > SLOTS and (f - SLOTS) % 2 == 1 and (f - SLOTS) // 2 < NC:
                        gather_pool(pool, g, nb, (f - SLOTS) // 2)
                for c in range(NC):
                    scatter_pool(pool, e, b, c)

        def load_weights(sp, e, f):
            n = e * KF + f
            wait(sp, w1_low, n - 1)
            sp.dma_start(raw1[:, f % 2, :, :], w1_v[e, :, :, f * P:(f + 1) * P] if isinstance(e, int) else
                         w1_v[bass.ds(e, 1), :, :, f * P:(f + 1) * P].rearrange("o p k f -> (o p) k f"))\
              .then_inc(w1_in[f % 2], 16)
            wait(sp, w2_low, n - 1)
            sp.dma_start(raw2[:, f % 2, :], w2_v[e, :, f, :] if isinstance(e, int) else
                         w2_v[bass.ds(e, 1), :, f, :].rearrange("o p d -> (o p) d"))\
              .then_inc(w2_in[f % 2], 16)

        CONSTS = 8
        DVE_OWN_ATTENTION = NQ * (4 + 3) * 2 + NQ * 2

        @block.sync
        def _(sp):
            small = [(bias_rows[0:KD, :], bk.rearrange("(c p) -> c p", p=P)),
                     (bias_rows[KD:2 * KD, :], bv.rearrange("(c p) -> c p", p=P)),
                     (bias_rows[2 * KD:3 * KD, :], bq.rearrange("(c p) -> c p", p=P)),
                     (bo_row[:, :], bo.rearrange("(a d) -> a d", a=1)),
                     (gate_raw[:, :], gate_w)]
            sp.dma_start(raw_k[:, :, :], Wk.rearrange("(c p) e -> p c e", p=P)).then_inc(lin[2], 16)
            for dst, src in small:
                sp.dma_start(dst, src).then_inc(lin[0], 16)
            sp.dma_start(ctx_raw[:, :, :], ctx_in.rearrange("b j d -> j b d")).then_inc(lin[1], 16)
            sp.dma_start(x_s[:, 0, :, :], x_q[0]).then_inc(x_in[0], 16)
            sp.dma_start(raw_q[:, :, :], Wq.rearrange("(c p) e -> p c e", p=P)).then_inc(lin[3], 16)
            sp.dma_start(raw_v[:, :, :], Wv.rearrange("(c p) e -> p c e", p=P)).then_inc(lin[4], 16)
            sp.dma_start(x_s[:, 1, :, :], x_q[1]).then_inc(x_in[1], 16)
            sp.dma_start(raw_o[:, :, :], Wo.rearrange("(c p) e -> p c e", p=P)).then_inc(lin[5], 16)
            sp.dma_start(mask_i[:, :, :], mask_v).then_inc(mask_in, 16)
            sp.dma_start(x_s[:, 2, :, :], x_q[2]).then_inc(x_in[2], 16)
            for q in range(NQ):
                sp.wait_ge(added, Q * q + Q)
                sp.dma_start(out_q[q], x1[:, q % 2, :, :]).then_inc(x1_out[q % 2], 16)
                if q + 3 < NQ:
                    sp.dma_start(x_s[:, q % 3, :, :], x_q[q + 3]).then_inc(x_in[q % 3], 16)
                sp.wait_ge(normed2, Q * q + Q)
                sp.dma_start(xn_q[q], xn2[:, q % 2, :, :]).then_inc(xn_out[q % 2], 16)
            sp.wait_ge(logit_out, NQ)
            rows_stored(sp)
            for f in range(KF):
                load_weights(sp, 0, f)
            with sp.Fori(1, E) as e:
                for f in range(KF):
                    load_weights(sp, e, f)
            for c in range(NC):
                sp.wait_ge(scattered[c], 16 * G)

        @block.gpsimd
        def _(pool):
            pool.dma_start(gates_raw[:, 0:1], g_xattn.rearrange("(a o) -> a o", o=1).to_broadcast([P, 1]))\
                .then_inc(lin[6], 16)
            pool.dma_start(gates_raw[:, 1:2], g_ffn.rearrange("(a o) -> a o", o=1).to_broadcast([P, 1]))\
                .then_inc(lin[6], 16)
            pool.memset(ones_row[:, :], 1.0).then_inc(consts, 1)
            pool.memset(ident[:, :], 0.0).then_inc(pool_start, 1)
            pool.memset(powers[:, :], -0.5).then_inc(pool_start, 1)
            pool.wait_ge(pool_start, 2)
            pool.affine_select(out=ident[:, :], in_=ident[:, :], compare_op=ALU.not_equal, fill=1.0, base=0,
                               pattern=[[-1, P]], channel_multiplier=1).then_inc(consts, 1)
            attention_pool(pool)
            pool.wait_ge(logit_out, NQ)
            rows_stored(pool)
            pool.memset(ones_m[:, :], 1.0).then_inc(consts, 1)
            pool.memset(below_m[:, :], 1.0).then_inc(consts, 1)
            pool.wait_ge(consts, 4)
            pool.affine_select(out=below_m[:, :], in_=below_m[:, :], compare_op=ALU.is_gt, fill=0.0, base=0,
                               pattern=[[1, P]], channel_multiplier=-1).then_inc(consts, 1)
            pool.iota(vrow_i[:, :, :], pattern=[[1, NT]], base=0, channel_multiplier=0).then_inc(consts, 1)
            pool.iota(vpar_i[:, :], pattern=[[1, 1]], base=0, channel_multiplier=1).then_inc(consts, 1)
            pool.iota(iota_i[:, :], pattern=[[1, P]], base=0, channel_multiplier=0).then_inc(consts, 1)
            for f in range(KF - LAG):
                weight_low_pool(pool, 0, f)
            for c in range(NC):
                gather_pool(pool, 0, 0, c)
            expert_pool(pool, 0, False)
            with pool.Fori(1, E - 1) as e:
                expert_pool(pool, e, False)
            expert_pool(pool, E - 1, True)

        @block.scalar
        def _(act):
            act.wait_ge(lin[6], 32)
            act.activation(gates[:, :], gates_raw[:, :], ACT.Tanh).then_inc(gates_done, 1)
            prep_out(act, prep_act, True)
            attention_act(act)
            act.wait_ge(pdiff, 1)
            act.activation(flat(pexp), flat(prob), ACT.Exp).then_inc(pexped, 1)
            for f in range(KF - LAG):
                weight_high_act(act, 0, f)
            gelu_act(act, 0, 0, 0)
            expert_act(act, 0, False)
            with act.Fori(1, E - 1) as e:
                expert_act(act, e, False)
            expert_act(act, E - 1, True)

        @block.vector
        def _(dve):
            prep_out(dve, prep_dve, False)
            attention_dve(dve)
            choice_dve(dve, DVE_OWN_ATTENTION)
            hot_dve(dve, 0, 0, 0)
            slots_dve(dve, 0, 0)
            for c in range(NC):
                split_tokens_dve(dve, 0, 0, c)
            split_hidden_dve(dve, 0, 0, 0)
            expert_dve(dve, 0, False)
            with dve.Fori(1, E - 1) as e:
                expert_dve(dve, e, False)
            expert_dve(dve, E - 1, True)

        @block.tensor
        def _(pe):
            prep_pe(pe)
            attention_pe(pe)
            choice_pe(pe)
            slots_pe(pe, 0)
            for c in range(NC):
                tokens_pe(pe, 0, c)
            hidden_pe(pe, 0, 0, 0)
            expert_pe(pe, 0, False)
            with pe.Fori(1, E - 1) as e:
                expert_pe(pe, e, False)
            expert_pe(pe, E - 1, True)


INPUTS = ["x", "ctx_1024", "mask_BxSxS2_ik0", "g_xattn", "g_ffn", "L0_xattn_Wq", "L0_xattn_bq", "L0_xattn_Wk",
          "L0_xattn_bk", "L0_xattn_Wv", "L0_xattn_bv", "L0_xattn_Wo", "L0_xattn_bo", "L0_ffn_gate_w", "L0_ffn_w1",
          "L0_ffn_w2"]


def kernel(**inputs):
    import concourse.bacc as bacc
    from concourse.bass_utils import run_bass_kernel_spmd

    nc = bacc.Bacc("TRN2", target_bir_lowering=False, num_devices=1)
    arrays, args = {}, []
    for name in INPUTS:
        a = np.ascontiguousarray(inputs[name])
        arrays[f"in_{name}"] = a
        args.append(nc.dram_tensor(f"in_{name}", a.shape, mybir.dt.from_np(a.dtype), kind="ExternalInput").ap())
    shape = inputs["x"].shape
    args.append(nc.dram_tensor("layer_out", shape, F32, kind="ExternalOutput").ap())
    flamingo_layer(nc, *args)
    r = run_bass_kernel_spmd(nc, [arrays], core_ids=[0])
    return r.results[0]["layer_out"]
```

```python
from contextlib import ExitStack

import numpy as np

import concourse.bass as bass
from concourse import mybir

F32 = mybir.dt.float32
F32R = mybir.dt.float32r
BF16 = mybir.dt.bfloat16
I32 = mybir.dt.int32
U32 = mybir.dt.uint32
ALU = mybir.AluOpType
ACT = mybir.ActivationFunctionType
AX = mybir.AxisListType

P = 128
BANK = 512
EPS = 1e-5
MASKED = -1.0e30
BITS = 30
STEPS = BITS // 2


def wait(eng, sem, value):
    if not isinstance(value, int) or value > 0:
        eng.wait_ge(sem, value)


class Tally:

    def __init__(self, sem):
        self.sem, self.n = sem, 0

    def mark(self, ins):
        ins.then_inc(self.sem, 1)
        self.n += 1
        return self.n


def flamingo_layer(nc, x, ctx_in, mask, g_xattn, g_ffn, Wq, bq, Wk, bk, Wv, bv, Wo, bo, gate_w, w1, w2, out):
    B, S, D = x.shape
    J = ctx_in.shape[1]
    E, _, F = w1.shape
    CAP = 2 * S // E
    KD = D // P
    KF = F // P
    TB = S // P
    NT = B * TB
    Q = 4
    NQ = NT // Q
    QB = NQ // B
    NC = CAP // P
    G = B * E
    BJ = B * J
    JE = J + E
    NV = 5
    SCALE = float(D) ** -0.5
    assert JE <= P and D == BANK and CAP == BANK and J <= P and KD == NC == 4 and KF == 16 and B == 2 and E == 8

    x_q = x.rearrange("b (q i p) d -> (b q) p i d", i=Q, p=P)
    out_rows = out.rearrange("b s d -> (b s) d")
    out_q = out_rows.rearrange("(q i p) d -> q p i d", i=Q, p=P)
    xn_rows = nc.dram_tensor("xn_rows", [B * S, D], F32, kind="Internal").ap()
    xn_q = xn_rows.rearrange("(q i p) d -> q p i d", i=Q, p=P)
    mask_v = mask.rearrange("b (t p) j -> p (b t) j", p=P)
    w1_v = w1.rearrange("e (k p) f -> e p k f", p=P)
    w2_v = w2.rearrange("e (c p) d -> e p c d", p=P)

    whole = ExitStack()
    with whole:
        def sem(name):
            return whole.enter_context(nc.semaphore(name))

        def keep(name, shape, dt):
            return whole.enter_context(nc.sbuf_tensor(name, shape, dt))

        bank = [whole.enter_context(nc.psum_tensor(f"bank{i}", [P, BANK], F32)) for i in range(8)]

        ident = keep("ident", [P, P], F32)
        iota_slot = keep("iota_slot", [P, P], BF16)
        iota_block = keep("iota_block", [P, NC], BF16)
        slot_lo = keep("slot_lo", [P, B, TB, E], BF16)
        slot_hi = keep("slot_hi", [P, B, TB, E], BF16)
        values = keep("values", [P, B, TB, E, NV], BF16)
        gates = keep("gates", [P, 2], F32)
        logits = keep("logits", [P, B, TB, E], F32)

        chooser = ExitStack()

        def choice(name, dt, shape=(P, TB, E)):
            return chooser.enter_context(nc.sbuf_tensor(name, list(shape), dt))

        with chooser:
            prob = choice("prob", F32)
            pexp = choice("pexp", F32)
            pstat = choice("pstat", F32, (P, 3, TB))
            ones_m = choice("ones_m", BF16, (P, P))
            below_m = choice("below_m", BF16, (P, P))
            bit_table = choice("bit_table", I32, (P, STEPS, 3, E))
            cand = choice("cand", I32, (P, 3, E))
            found = choice("found", F32, (P, 2, 4, E))
            atleast = choice("atleast", BF16, (P, 3, TB, E))
            count = choice("count", BF16, (P, 3, E))
            above = choice("above", BF16)
            tied = choice("tied", BF16)
            need = choice("need", F32, (P, E))
            chosen = choice("chosen", BF16)
            fits = choice("fits", BF16)
            place_i = choice("place_i", I32)
            part_i = choice("part_i", I32)
        y = keep("y", [P, NC, D], F32)

        early = ExitStack()

        def first(name, shape, dt):
            return early.enter_context(nc.sbuf_tensor(name, shape, dt))

        with early:
            gates_raw = first("gates_raw", [P, 2], F32)
            mean_m = first("mean_m", [P, P], F32)
            bias_rows = first("bias_rows", [3 * KD, P], F32)
            bo_all = first("bo_all", [J, D], F32)
            gate_raw = first("gate_raw", [E, D], F32)
            cols = first("cols", [P, 3 * KD + KD * E], F32)
            ctx_raw = first("ctx_raw", [J, B, D], F32)
            raw_k, raw_q, raw_v, raw_o, wkT, wvT, woT = (
                first(n, [P, KD, D], F32) for n in ("raw_k", "raw_q", "raw_v", "raw_o", "wkT", "wvT", "woT"))
            ctxT = first("ctxT", [P, KD, B, J], F32)
            kT = first("kT", [P, KD, BJ], F32)
            vT = first("vT", [P, KD, BJ], F32)
            qkg = first("qkg", [P, KD, B, JE], F32)
            qkc = first("qkc", [P, KD, B, JE], F32)
            cb = first("cb", [P, B, J], F32)
            vo = first("vo", [P, B, D], F32)
            voT = first("voT", [P, KD, B, J], F32)
            vg = first("vg", [P, B, E], F32)
            mask_i = first("mask_i", [P, NT, J], I32)
            x_s = first("x_s", [P, 3, Q, D], F32)
            xT = first("xT", [P, 2, KD, Q * P], F32)
            sT = first("sT", [JE, 2, Q * P], F32)
            mflag = first("mflag", [P, Q, J], F32)
            mbias = first("mbias", [P, 2, Q, J], F32)
            sc = first("sc", [P, 2, Q, J], F32)
            ex = first("ex", [P, 2, Q, J], F32)
            eT = first("eT", [P, 2, Q * P], F32)
            x1 = first("x1", [P, 2, Q, D], F32)
            xn2 = first("xn2", [P, 2, Q, D], F32)
            st2 = first("st2", [P, Q, 6], F32)
            mv2 = first("mv2", [P, 2, Q, 2], F32)
            norm1 = first("norm1", [P, 2, 2, Q], F32)
            spare = first("spare", [P, Q, D], BF16)
            xsum = first("xsum", [P, 2, Q], F32)
            xmean = first("xmean", [P, 2, Q], F32)
            xvar = first("xvar", [P, 2, Q], F32)
            norm2 = first("norm2", [P, 2, 4, Q], F32)
            powers = first("powers", [P, Q], F32)
            smax = first("smax", [P, 2, Q], F32)
            smaxn = first("smaxn", [P, 2, Q], F32)
            rsum = first("rsum", [P, 2, Q], F32)
            rinv = first("rinv", [P, 2, Q], F32)
            xg1 = first("xg1", [P, 2, Q, E], F32)
            lg1 = first("lg1", [P, 2, Q, E], F32)
            vrow_i = first("vrow_i", [P, NT], I32)
            vpar_i = first("vpar_i", [P, 1], I32)
            iota_i = first("iota_i", [P, P], I32)

        w1h = keep("w1h", [P, KF, KD, P], F32R)
        w1l = keep("w1l", [P, KF, KD, P], F32R)
        w2h = keep("w2h", [P, KF, D], F32R)
        w2l = keep("w2l", [P, KF, D], F32R)
        raw1 = keep("raw1", [P, 2, KD, P], F32)
        raw2 = keep("raw2", [P, 2, D], F32)

        xTh = keep("xTh", [P, B, KD, CAP], F32R)
        xTl = keep("xTl", [P, B, KD, CAP], F32R)
        hf = keep("hf", [P, 2, CAP], F32)
        hh = keep("hh", [P, 2, CAP], F32R)
        hl = keep("hl", [P, 2, CAP], F32R)
        xg = keep("xg", [P, NC, D], F32)
        spare_gate = keep("spare_gate", [P, 1], F32)
        onehot = keep("onehot", [P, TB, P], BF16)
        blockhot = keep("blockhot", [P, TB, NC], BF16)
        carried = keep("carried", [P, TB, NC, NV], BF16)
        got = keep("got", [P, NC, NV], F32)
        slot_gate = keep("slot_gate", [P, B, 2, NC], F32)
        slot_row = keep("slot_row", [P, B, NC], U32)

        consts = sem("consts")
        pool_start = sem("pool_start")
        lin = [sem(f"lin{i}") for i in range(7)]
        prep_full = sem("prep_full")
        prep_act = sem("prep_act")
        prep_dve = sem("prep_dve")
        gates_done = sem("gates_done")
        vo_sum = sem("vo_sum")
        x_in = [sem(f"x_in{i}") for i in range(3)]
        mask_in = sem("mask_in")
        x_summed = sem("x_summed")
        mean_ready = sem("mean_ready")
        stats1 = sem("stats1")
        stats2 = sem("stats2")
        pool_own = sem("pool_own")
        dve_own = sem("dve_own")
        normed1 = sem("normed1")
        deviated2 = sem("deviated2")
        normed2 = sem("normed2")
        turned = sem("turned")
        turn_out = sem("turn_out")
        scored = sem("scored")
        mask_ready = sem("mask_ready")
        sc_ready = sem("sc_ready")
        smax_ready = sem("smax_ready")
        exped = sem("exped")
        weighed = sem("weighed")
        routed = sem("routed")
        added = sem("added")
        logit_out = sem("logit_out")
        x1_out = [sem(f"x1_out{i}") for i in range(2)]
        xn_out = [sem(f"xn_out{i}") for i in range(2)]

        pdiff = sem("pdiff")
        pexped = sem("pexped")
        bit_count = sem("bit_count")
        bit_total = sem("bit_total")
        pick_in = sem("pick_in")
        pick_sum = sem("pick_sum")
        chosen_all = sem("chosen_all")
        iotas = sem("iotas")

        w1_in = [sem(f"w1_in{i}") for i in range(2)]
        w2_in = [sem(f"w2_in{i}") for i in range(2)]
        w1_high = sem("w1_high")
        w2_high = sem("w2_high")
        w1_low = sem("w1_low")
        w2_low = sem("w2_low")
        hot = sem("hot")
        slots_sum = sem("slots_sum")
        slots_got = sem("slots_got")
        slots_own = sem("slots_own")
        slots_ready = sem("slots_ready")
        gathered = [sem(f"gathered{i}") for i in range(NC)]
        gathers = sem("gathers")
        scatters = sem("scatters")
        x_turned = sem("x_turned")
        x_high = sem("x_high")
        x_split = sem("x_split")
        h_sum = sem("h_sum")
        h_act = sem("h_act")
        h_high = sem("h_high")
        h_split = sem("h_split")
        y_sum = sem("y_sum")
        y_act = sem("y_act")
        y_dve = sem("y_dve")
        scattered = [sem(f"scattered{i}") for i in range(NC)]

        block = whole.enter_context(nc.Block())

        steps = [("cols", 0, None)]
        steps += [("ctx", b, None) for b in range(B)]
        steps += [("turn_k", k, None) for k in range(KD)]
        steps += [("kT", h, 6) for h in range(2)]
        steps += [("cb", 0, 8)]
        steps += [("qk", h, 8) for h in range(2)]
        steps += [("turn_v", 0, None), ("mean", 0, 11)]
        steps += [("turn_v", k, None) for k in range(1, KD)]
        steps += [("vT", h, 16) for h in range(2)]
        steps += [("turn_o", k, None) for k in range(KD)]
        steps += [("vo", 0, 22), ("voT", 0, 23), ("vo", 1, 24), ("voT", 1, 25), ("vg", 0, 26)]
        BC = 3 * KD
        needs_in = {"cols": (0, 5 * 16), "ctx": (1, 16), "turn_k": (2, 16), "qk": (3, 16), "turn_v": (4, 16),
                    "turn_o": (5, 16)}

        def wait_evacuated(eng, n):
            eng.wait_ge(prep_act, n // 2 + 1)
            if n >= 1:
                eng.wait_ge(prep_dve, (n + 1) // 2)

        def prep_pe(pe):
            pe.wait_ge(consts, 1)
            for n, (name, i, after) in enumerate(steps):
                bk = bank[n % 2]
                if name in needs_in:
                    which, value = needs_in[name]
                    pe.wait_ge(lin[which], value)
                if n >= 2:
                    pe.wait_ge(prep_act if n % 2 == 0 else prep_dve, n // 2)
                if after is not None:
                    wait_evacuated(pe, after)
                if name == "cols":
                    pe.transpose(bk[:, 0:BC], bias_rows[:, :], ident[0:BC, 0:BC])
                    for k in range(KD):
                        last = pe.transpose(bk[:, BC + k * E:BC + (k + 1) * E], gate_raw[:, k * P:(k + 1) * P],
                                            ident[0:E, 0:E])
                elif name == "ctx":
                    for k in range(KD):
                        last = pe.transpose(bk[:, k * J:(k + 1) * J], ctx_raw[:, i, k * P:(k + 1) * P],
                                            ident[0:J, 0:J])
                elif name.startswith("turn"):
                    raw_w = {"turn_k": raw_k, "turn_v": raw_v, "turn_o": raw_o}[name]
                    for c in range(KD):
                        last = pe.transpose(bk[:, c * P:(c + 1) * P], raw_w[:, c, i * P:(i + 1) * P], ident[:, :])
                elif name in ("kT", "vT"):
                    wt = wkT if name == "kT" else wvT
                    for h in range(2):
                        for k in range(KD):
                            c = 2 * i + h
                            last = pe.matmul(bk[:, h * BJ:(h + 1) * BJ], wt[:, k, c * P:(c + 1) * P],
                                             ctxT[:, k, :, :].rearrange("p b j -> p (b j)"),
                                             start=(k == 0), stop=(k == KD - 1))
                elif name == "cb":
                    for c in range(KD):
                        last = pe.matmul(bk[:, 0:BJ], cols[:, 2 * KD + c:2 * KD + c + 1].to_broadcast([P, P]),
                                         kT[:, c, :], start=(c == 0), stop=(c == KD - 1))
                elif name == "mean":
                    pe.wait_ge(consts, 2)
                    for d in range(KD):
                        last = pe.matmul(bk[:, 0:B * JE], mean_m[:, :], qkg[:, d, :, :].rearrange("p b j -> p (b j)"),
                                         start=(d == 0), stop=(d == KD - 1))
                elif name == "qk":
                    for h in range(2):
                        for c in range(KD):
                            d = 2 * i + h
                            last = pe.matmul(bk[:, h * BJ:(h + 1) * BJ], raw_q[:, c, d * P:(d + 1) * P], kT[:, c, :],
                                             start=(c == 0), stop=(c == KD - 1))
                elif name == "vo":
                    for c in range(KD):
                        last = pe.matmul(bk[0:J, :], vT[:, c, i * J:(i + 1) * J], woT[:, c, :], start=(c == 0),
                                         stop=(c == KD - 1))
                elif name == "voT":
                    for k in range(KD):
                        last = pe.transpose(bk[:, k * J:(k + 1) * J], vo[0:J, i, k * P:(k + 1) * P],
                                            ident[0:J, 0:J])
                elif name == "vg":
                    for b in range(B):
                        for k in range(KD):
                            last = pe.matmul(bk[0:J, b * E:(b + 1) * E], voT[:, k, b, :], qkc[:, k, b, J:JE],
                                             start=(k == 0), stop=(k == KD - 1))
                last.then_inc(prep_full, 1)

        def prep_out(eng, mine, is_act):
            def copy(dst, src, scale=None, bias=None):
                if is_act:
                    if bias is not None:
                        return eng.activation(dst, src, ACT.Identity, bias=bias)
                    return eng.activation(dst, src, ACT.Copy, scale=1.0 if scale is None else scale)
                if bias is not None:
                    return eng.tensor_scalar(dst, src, bias, None, ALU.add)
                if scale is not None:
                    return eng.tensor_scalar(dst, src, scale, None, ALU.mult)
                return eng.tensor_copy(dst, src)

            for n, (name, i, _) in enumerate(steps):
                if (n % 2 == 0) != is_act:
                    continue
                bk = bank[n % 2]
                eng.wait_ge(prep_full, n + 1)
                if name == "cols":
                    last = copy(cols[:, :], bk[:, 0:BC + KD * E])
                elif name == "ctx":
                    last = copy(ctxT[:, :, i, :], bk[:, 0:KD * J].rearrange("p (k j) -> p k j", k=KD))
                elif name == "turn_k":
                    last = copy(wkT[:, i, :], bk[:, :])
                elif name == "turn_v":
                    last = copy(wvT[:, i, :], bk[:, :])
                elif name == "turn_o":
                    last = copy(woT[:, i, :], bk[:, :])
                elif name in ("kT", "vT"):
                    eng.wait_ge(prep_act, 1)
                    for h in range(2):
                        c = 2 * i + h
                        at = c + (0 if name == "kT" else KD)
                        last = copy((kT if name == "kT" else vT)[:, c, :], bk[:, h * BJ:(h + 1) * BJ],
                                    bias=cols[:, at:at + 1])
                elif name == "cb":
                    last = copy(cb[:, :, :].rearrange("p b j -> p (b j)"), bk[:, 0:BJ], scale=SCALE)
                elif name == "qk":
                    for h in range(2):
                        last = copy(qkg[:, 2 * i + h, :, 0:J],
                                    bk[:, h * BJ:(h + 1) * BJ].rearrange("p (b j) -> p b j", b=B), scale=SCALE)
                    if not is_act:
                        eng.wait_ge(prep_act, 1)
                        for b in range(B):
                            last = copy(qkg[:, :, b, J:JE], cols[:, BC:BC + KD * E].rearrange("p (k e) -> p k e", k=KD))
                elif name == "mean":
                    eng.wait_ge(prep_act, 6)
                    eng.wait_ge(prep_dve, 6)
                    last = eng.tensor_tensor(qkc[:, :, :, :].rearrange("p k b j -> p k (b j)"),
                                             qkg[:, :, :, :].rearrange("p k b j -> p k (b j)"),
                                             bk[:, 0:B * JE].unsqueeze(1).to_broadcast([P, KD, B * JE]), ALU.subtract)
                elif name == "vo":
                    eng.wait_ge(gates_done, 1)
                    eng.wait_ge(consts, 3)
                    eng.tensor_tensor(vo[0:J, i, :], bk[0:J, :], bo_all[:, :], ALU.add).then_inc(vo_sum, 1)
                    eng.wait_ge(vo_sum, i + 1)
                    last = eng.tensor_scalar(vo[0:J, i, :], vo[0:J, i, :], gates[0:J, 0:1], None, ALU.mult)
                elif name == "voT":
                    last = copy(voT[:, :, i, :], bk[:, 0:KD * J].rearrange("p (k j) -> p k j", k=KD))
                elif name == "vg":
                    last = copy(vg[0:J, :, :], bk[0:J, 0:B * E].rearrange("p (b e) -> p b e", b=B))
                last.then_inc(mine, 1)

        turns = []
        for it in range(NQ + 1):
            turns += [("x", it, i) for i in range(Q) if it < NQ]
            turns += [("e", it - 1, 0)] if it >= 1 else []
            turns += [("s", it, 0)] if it < NQ else []
        turn_at = {t: n for n, t in enumerate(turns)}
        T_BANKS = (2, 3, 4)
        O_BANKS = (bank[0], bank[1])
        SC_BANK, VG_BANK, CHOICE_BANK = bank[5], bank[6], bank[7]
        CHOOSE_FROM, PLACES = QB + 1, 4

        def turn_bank(turn):
            return bank[T_BANKS[turn_at[turn] % 3]]

        def pe_bank_free(pe, turn):
            wait(pe, turn_out, turn_at[turn] - 2)

        def attention_pe(pe, between):
            for it in range(NQ + 1):
                q = it
                if q < NQ:
                    pe.wait_ge(x_in[q % 3], 16 * (q // 3 + 1))
                    for i in range(Q):
                        pe_bank_free(pe, ("x", q, i))
                        for k in range(KD):
                            last = pe.transpose(turn_bank(("x", q, i))[:, k * P:(k + 1) * P],
                                                x_s[:, q % 3, i, k * P:(k + 1) * P], ident[:, :])
                        last.then_inc(turned, 1)
                        if i == 1:
                            between(it - 1, 2)
                else:
                    between(it - 1, 2)
                q = it - 1
                if q >= 0:
                    pe.wait_ge(exped, q + 1)
                    pe_bank_free(pe, ("e", q, 0))
                    for i in range(Q):
                        last = pe.transpose(turn_bank(("e", q, 0))[0:J, i * P:(i + 1) * P], ex[:, q % 2, i, :],
                                            ident[:, :])
                    last.then_inc(turned, 1)
                between(it - 1, 3)
                q = it
                if q < NQ:
                    b = q // QB
                    if q == 0:
                        wait_evacuated(pe, 13)
                    pe_bank_free(pe, ("s", q, 0))
                    pe.wait_ge(turn_out, turn_at["x", q, Q - 1] + 1)
                    for k in range(KD):
                        last = pe.matmul(turn_bank(("s", q, 0))[0:JE, :], qkc[:, k, b, :], xT[:, q % 2, k, :],
                                         start=(k == 0), stop=(k == KD - 1))
                        if k == 1:
                            between(it, 0)
                    last.then_inc(turned, 1)
                else:
                    between(it, 0)
                between(it, 1)
                for i in range(Q):
                    q = it - 1
                    if q >= 0:
                        b = q // QB
                        if i == 0:
                            if q == 0:
                                wait_evacuated(pe, len(steps) - 1)
                            pe.wait_ge(turn_out, turn_at["e", q, 0] + 1)
                            wait(pe, logit_out, q)
                        n = Q * q + i
                        wait(pe, added, n - 1)
                        pe.matmul(O_BANKS[n % 2][:, :], eT[:, q % 2, i * P:(i + 1) * P], vo[:, b, :],
                                  start=True, stop=True).then_inc(weighed, 1)
                        last = pe.matmul(VG_BANK[:, i * E:(i + 1) * E], eT[:, q % 2, i * P:(i + 1) * P], vg[:, b, :],
                                         start=True, stop=True)
                        if i == Q - 1:
                            last.then_inc(routed, 1)
                    q = it
                    if i == 0 and q < NQ:
                        pe.wait_ge(turn_out, turn_at["s", q, 0] + 1)
                        wait(pe, sc_ready, q)
                        for t in range(Q):
                            last = pe.transpose(SC_BANK[:, t * JE:(t + 1) * JE], sT[:, q % 2, t * P:(t + 1) * P],
                                                ident[0:JE, 0:JE])
                        last.then_inc(scored, 1)
            for it, place in ((NQ, 2), (NQ, 3), (NQ + 1, 0), (NQ + 1, 1), (NQ + 1, 2), (NQ + 1, 3)):
                between(it, place)

        def attention_act(act):
            def sums(q):
                act.wait_ge(x_in[q % 3], 16 * (q // 3 + 1))
                wait(act, stats1, q)
                for i in range(Q):
                    last = act.activation(spare[:, i, :], x_s[:, q % 3, i, :], ACT.Copy,
                                          accum_out=xsum[:, q % 2, i:i + 1])
                last.then_inc(x_summed, 1)
                act.wait_ge(x_summed, q + 1)
                act.activation(xmean[:, q % 2, :], xsum[:, q % 2, :], ACT.Copy, scale=-1.0 / D).then_inc(mean_ready, 1)

            def squares(q):
                act.wait_ge(mean_ready, q + 1)
                wait(act, normed1, q - 1)
                for i in range(Q):
                    last = act.activation(spare[:, i, :], x_s[:, q % 3, i, :], ACT.Square,
                                          bias=xmean[:, q % 2, i:i + 1], accum_out=xvar[:, q % 2, i:i + 1])
                last.then_inc(stats1, 1)

            sums(0)
            for it in range(NQ + 1):
                q = it
                if q < NQ:
                    for i in range(Q):
                        act.wait_ge(turned, turn_at["x", q, i] + 1)
                        if q >= 2:
                            act.wait_ge(turned, turn_at["s", q - 2, 0] + 1)
                        act.activation(xT[:, q % 2, :, i * P:(i + 1) * P],
                                       turn_bank(("x", q, i))[:, :].rearrange("p (k t) -> p k t", k=KD), ACT.Copy)\
                           .then_inc(turn_out, 1)
                q = it - 1
                if q >= 0:
                    act.wait_ge(turned, turn_at["e", q, 0] + 1)
                    wait(act, routed, q - 1)
                    act.wait_ge(consts, 3)
                    act.activation(eT[0:J, q % 2, :], turn_bank(("e", q, 0))[0:J, :], ACT.Copy).then_inc(turn_out, 1)
                q = it
                if q < NQ:
                    squares(q)
                    act.wait_ge(turned, turn_at["s", q, 0] + 1)
                    wait(act, scored, q - 1)
                    act.activation(sT[:, q % 2, :], turn_bank(("s", q, 0))[0:JE, :], ACT.Copy).then_inc(turn_out, 1)
                    if q + 1 < NQ:
                        sums(q + 1)
                    act.wait_ge(smax_ready, q + 1)
                    if q >= 2:
                        act.wait_ge(turned, turn_at["e", q - 2, 0] + 1)
                        act.wait_ge(added, Q * (q - 1))
                    for i in range(Q):
                        last = act.activation(ex[:, q % 2, i, :], sc[:, q % 2, i, :], ACT.Exp,
                                              bias=smaxn[:, q % 2, i:i + 1], accum_out=rsum[:, q % 2, i:i + 1])
                    last.then_inc(exped, 1)
                if it == CHOOSE_FROM:
                    choice_act(act, 0)

        def attention_pool(pool):
            own = Tally(pool_own)

            def first_deviations(q):
                s = q % 2
                pool.wait_ge(stats1, q + 1)
                own.mark(pool.tensor_scalar(norm1[:, s, 0, :], xvar[:, s, :], 1.0 / D, EPS, ALU.mult, ALU.add))
                pool.wait_ge(pool_own, own.n)
                pool.tensor_tensor(norm1[:, s, 1, :], norm1[:, s, 0, :], powers[:, :], ALU.pow).then_inc(normed1, 1)

            def second_deviations(q):
                mv, nm, s = mv2, norm2, q % 2
                own.mark(pool.tensor_scalar(nm[:, s, 0, :], mv[:, s, :, 1], EPS, None, ALU.add))
                own.mark(pool.tensor_scalar(nm[:, s, 1, :], mv[:, s, :, 0], -1.0, None, ALU.mult))
                pool.wait_ge(pool_own, own.n)
                pool.tensor_tensor(nm[:, s, 2, :], nm[:, s, 0, :], powers[:, :], ALU.pow).then_inc(deviated2, 1)
                pool.wait_ge(deviated2, q + 1)
                own.mark(pool.tensor_tensor(nm[:, s, 3, :], nm[:, s, 1, :], nm[:, s, 2, :], ALU.mult))
                pool.wait_ge(pool_own, own.n)

            def mask_biases(q):
                if q == 0:
                    pool.wait_ge(mask_in, 16)
                    pool.wait_ge(prep_dve, 5)
                wait(pool, sc_ready, q - 1)
                wait(pool, mask_ready, q)
                own.mark(pool.tensor_scalar(mflag[:, :, :], mask_i[:, Q * q:Q * q + Q, :], 0.0, MASKED,
                                            ALU.is_equal, ALU.mult))
                pool.wait_ge(pool_own, own.n)
                pool.tensor_tensor(mbias[:, q % 2, :, :], mflag[:, :, :],
                                   cb[:, q // QB, :].unsqueeze(1).to_broadcast([P, Q, J]), ALU.add)\
                    .then_inc(mask_ready, 1)

            mask_biases(0)
            first_deviations(0)
            for it in range(NQ + 1):
                if it + 1 < NQ:
                    mask_biases(it + 1)
                if it == 0:
                    first_deviations(1)
                q = it - 1
                if q >= 0:
                    pool.wait_ge(stats2, q + 1)
                    if q >= 2:
                        pool.wait_ge(logit_out, q - 1)
                        pool.wait_ge(xn_out[q % 2], 16 * (q // 2))
                    second_deviations(q)
                    for i in range(Q):
                        if i == Q // 2 and it + 1 < NQ:
                            first_deviations(it + 1)
                        pool.tensor_scalar(xn2[:, q % 2, i, :], x1[:, q % 2, i, :], norm2[:, q % 2, 2, i:i + 1],
                                           norm2[:, q % 2, 3, i:i + 1], ALU.mult, ALU.add).then_inc(normed2, 1)

        def attention_dve(dve, own, between):
            def step(ins):
                own.mark(ins)
                dve.wait_ge(dve_own, own.n)

            def logits_out(q):
                s = q % 2
                dve.wait_ge(routed, q + 1)
                step(dve.tensor_tensor(lg1[:, 0, :, :], VG_BANK[:, 0:Q * E].rearrange("p (i e) -> p i e", i=Q),
                                       rinv[:, s, :].unsqueeze(2).to_broadcast([P, Q, E]), ALU.mult))
                step(dve.tensor_tensor(lg1[:, 1, :, :], lg1[:, 0, :, :], xg1[:, s, :, :], ALU.add))
                dve.wait_ge(deviated2, q + 1)
                dve.tensor_tensor(logits[:, q // QB, (q % QB) * Q:(q % QB) * Q + Q, :], lg1[:, 1, :, :],
                                  norm2[:, s, 2, :].unsqueeze(2).to_broadcast([P, Q, E]), ALU.mult)\
                   .then_inc(logit_out, 1)

            def weigh(q, i):
                n = Q * q + i
                if i == 0:
                    dve.wait_ge(exped, q + 1)
                    step(dve.reciprocal(rinv[:, q % 2, :], rsum[:, q % 2, :]))
                    if q >= 2:
                        dve.wait_ge(x1_out[q % 2], 16 * (q // 2))
                        dve.wait_ge(normed2, Q * (q - 1))
                dve.wait_ge(weighed, n + 1)
                dve.scalar_tensor_tensor(out=x1[:, q % 2, i, :], in0=O_BANKS[n % 2][:, :],
                                         scalar=rinv[:, q % 2, i:i + 1], in1=x_s[:, q % 3, i, :],
                                         op0=ALU.mult, op1=ALU.add).then_inc(added, 1)

            for it in range(NQ + 2):
                for place in (0, 1):
                    between(it, place)
                if it >= 2:
                    logits_out(it - 2)
                if 0 <= it - 1 < NQ:
                    weigh(it - 1, 0)
                q = it
                if q < NQ:
                    bk = SC_BANK[:, 0:Q * JE].rearrange("p (i j) -> p i j", i=Q)
                    dve.wait_ge(scored, q + 1)
                    dve.wait_ge(normed1, q + 1)
                    dve.wait_ge(mask_ready, q + 1)
                    if q >= 1:
                        dve.wait_ge(exped, q)
                    own.mark(dve.tensor_copy(xg1[:, q % 2, :, :], bk[:, :, J:JE]))
                    for i in range(Q):
                        last = dve.scalar_tensor_tensor(out=sc[:, q % 2, i, :], in0=bk[:, i, 0:J],
                                                        scalar=norm1[:, q % 2, 1, i:i + 1],
                                                        in1=mbias[:, q % 2, i, :], op0=ALU.mult, op1=ALU.add)
                        own.mark(last) if i < Q - 1 else last.then_inc(sc_ready, 1)
                    dve.wait_ge(sc_ready, q + 1)
                    dve.wait_ge(dve_own, own.n)
                    step(dve.tensor_reduce(smax[:, q % 2, :], sc[:, q % 2, :, :], AX.X, ALU.max))
                    dve.tensor_scalar(smaxn[:, q % 2, :], smax[:, q % 2, :], -1.0, None, ALU.mult)\
                       .then_inc(smax_ready, 1)
                q = it - 1
                if 0 <= q < NQ:
                    for i in range(1, Q):
                        weigh(q, i)
                between(it, 2)
                if 0 <= q < NQ:
                    if q >= 1:
                        dve.wait_ge(stats2, q)
                    for i in range(Q):
                        dve.wait_ge(added, Q * q + i + 1)
                        own.mark(dve.bn_stats(st2[:, i, :], x1[:, q % 2, i, :]))
                    dve.wait_ge(dve_own, own.n)
                    for i in range(Q):
                        last = dve.bn_aggr(mv2[:, q % 2, i, :], st2[:, i, :])
                        own.mark(last) if i < Q - 1 else last.then_inc(stats2, 1)
                between(it, 3)

        def rows_stored(eng):
            for i in range(2):
                eng.wait_ge(x1_out[i], 16 * (NQ // 2))
                eng.wait_ge(xn_out[i], 16 * (NQ // 2))

        NE = TB * E
        N_PIECES = STEPS + 3

        def flat(t):
            return t[:, :, :].rearrange("p t e -> p (t e)")

        def over_tiles(t):
            return t.unsqueeze(1).to_broadcast([P, TB, E])

        def tile_counts(dve, dst, flags):
            with nc.allow_low_precision(reason="counts up to 16"):
                return dve.tensor_reduce(dst, flags, AX.X, ALU.add)

        def choice_act(act, b):
            act.wait_ge(pdiff, b + 1)
            act.activation(flat(pexp), flat(prob), ACT.Exp).then_inc(pexped, 1)

        def choice_dve(dve, own, b, piece):
            def step(ins):
                own.mark(ins)
                dve.wait_ge(dve_own, own.n)

            over_e = [pstat[:, i, :].unsqueeze(2).to_broadcast([P, TB, E]) for i in range(3)]
            if piece == 0:
                dve.wait_ge(logit_out, QB * (b + 1))
                lg = logits[:, b, :, :]
                step(dve.tensor_reduce(pstat[:, 0, :], lg, AX.X, ALU.max))
                dve.tensor_tensor(prob[:, :, :], lg, over_e[0], ALU.subtract).then_inc(pdiff, 1)
                own.mark(dve.memset(found[:, 0, 3, :], 0.0))
                dve.wait_ge(pexped, b + 1)
                step(dve.tensor_reduce(pstat[:, 1, :], pexp[:, :, :], AX.X, ALU.add))
                step(dve.reciprocal(pstat[:, 2, :], pstat[:, 1, :]))
                step(dve.tensor_tensor(prob[:, :, :], pexp[:, :, :], over_e[2], ALU.mult))
            if 1 <= piece <= STEPS:
                s = piece - 1
                dve.wait_ge(bit_total, b * STEPS + s + 1)
                step(dve.scalar_tensor_tensor(out=found[:, s % 2, 0:3, :],
                                              in0=CHOICE_BANK[:, 0:3 * E].rearrange("p (c e) -> p c e", c=3),
                                              scalar=float(CAP), in1=cand[:, :, :].bitcast(F32),
                                              op0=ALU.is_ge, op1=ALU.mult))
                step(dve.tensor_reduce(found[:, 1 - s % 2, 3, :], found[:, s % 2, :, :].rearrange("p c e -> p e c"),
                                       AX.X, ALU.max))
            thr = found[:, STEPS % 2, 3, :]
            if piece < STEPS:
                s = piece
                step(dve.tensor_tensor(cand[:, :, :], bit_table[:, s, :, :],
                                       found[:, s % 2, 3, :].bitcast(I32).unsqueeze(1).to_broadcast([P, 3, E]),
                                       ALU.bitwise_or))
                reach = dve.tensor_tensor(atleast[:, :, :, :], prob[:, :, :].unsqueeze(1).to_broadcast([P, 3, TB, E]),
                                          cand[:, :, :].bitcast(F32).unsqueeze(2).to_broadcast([P, 3, TB, E]),
                                          ALU.is_ge)
                if b == 0:
                    reach.then_inc(bit_count, 1)
                else:
                    step(reach)
                if b == 1:
                    tile_counts(dve, count[:, :, :], atleast[:, :, :, :].rearrange("p c t e -> p c e t"))\
                        .then_inc(bit_count, 1)
            elif piece == STEPS:
                step(dve.tensor_tensor(above[:, :, :], prob[:, :, :], over_tiles(thr), ALU.is_gt))
                step(dve.tensor_tensor(tied[:, :, :], prob[:, :, :], over_tiles(thr), ALU.is_equal))
                tile_counts(dve, count[:, 0, :], above[:, :, :].rearrange("p t e -> p e t")).then_inc(pick_in, 1)
                vals = values[:, b, :, :, :]
                step(dve.tensor_scalar(prob[:, :, :], prob[:, :, :], gates[:, 1:2], None, ALU.mult))
                step(dve.tensor_copy(vals[:, :, :, 2], prob[:, :, :]))
                step(dve.tensor_tensor(pexp[:, :, :], prob[:, :, :], vals[:, :, :, 2], ALU.subtract))
                step(dve.tensor_copy(vals[:, :, :, 3], pexp[:, :, :]))
            elif piece == STEPS + 1:
                dve.wait_ge(pick_sum, 2 * b + 1)
                step(dve.tensor_scalar(need[:, :], CHOICE_BANK[:, NE:NE + E], -1.0, float(CAP), ALU.mult, ALU.add))
                step(dve.tensor_tensor(fits[:, :, :], CHOICE_BANK[:, 0:NE].rearrange("p (t e) -> p t e", t=TB),
                                       over_tiles(need[:, :]), ALU.is_lt))
                step(dve.tensor_tensor(fits[:, :, :], fits[:, :, :], tied[:, :, :], ALU.mult))
                dve.tensor_tensor(chosen[:, :, :], above[:, :, :], fits[:, :, :], ALU.add).then_inc(pick_in, 1)
                vals = values[:, b, :, :, :]
                step(dve.tensor_tensor(vals[:, :, :, 4], pexp[:, :, :], vals[:, :, :, 3], ALU.subtract))
                dve.wait_ge(pick_in, 2 * b + 2)
            elif piece == STEPS + 2:
                dve.wait_ge(pick_sum, 2 * b + 2)
                step(dve.tensor_copy(flat(place_i), CHOICE_BANK[:, 0:NE]))
                step(dve.tensor_scalar(flat(part_i), flat(place_i), P - 1, None, ALU.bitwise_and))
                step(dve.tensor_copy(slot_lo[:, b, :, :], part_i[:, :, :]))
                step(dve.tensor_scalar(flat(part_i), flat(place_i), 7, None, ALU.logical_shift_right))
                dve.scalar_tensor_tensor(out=slot_hi[:, b, :, :], in0=part_i[:, :, :], scalar=1.0,
                                         in1=chosen[:, :, :], op0=ALU.add, op1=ALU.mult).then_inc(chosen_all, 1)
                dve.wait_ge(chosen_all, b + 1)

        def running_place(pe, flags):
            d, f = CHOICE_BANK[:, 0:NE], flat(flags)
            for s in range(1, TB):
                pe.matmul(d[:, s * E:], ones_m[:, :], f[:, 0:(TB - s) * E], start=(s == 1), stop=False,
                          skip_group_check=True)
            return pe.matmul(d, below_m[:, :], f, start=False, stop=True, skip_group_check=True)

        def choice_pe(pe, b, piece):
            if piece < STEPS:
                if b == 0 and piece == 0:
                    pe.wait_ge(consts, CONSTS)
                pe.wait_ge(bit_count, b * STEPS + piece + 1)
                total = CHOICE_BANK[:, 0:3 * E]
                if b == 0:
                    for t in range(TB):
                        last = pe.matmul(total.rearrange("p (c e) -> p c e", c=3), ones_m[:, :], atleast[:, :, t, :],
                                         start=(t == 0), stop=(t == TB - 1))
                else:
                    last = pe.matmul(total, ones_m[:, :], count[:, :, :].rearrange("p c e -> p (c e)"),
                                     start=True, stop=True)
                last.then_inc(bit_total, 1)
            elif piece == STEPS:
                pe.wait_ge(pick_in, 2 * b + 1)
                running_place(pe, tied)
                pe.matmul(CHOICE_BANK[:, NE:NE + E], ones_m[:, :], count[:, 0, :], start=True, stop=True)\
                  .then_inc(pick_sum, 1)
            elif piece == STEPS + 1:
                pe.wait_ge(pick_in, 2 * b + 2)
                running_place(pe, chosen).then_inc(pick_sum, 1)

        def beside_attention(do):
            def between(it, place):
                at = (it - CHOOSE_FROM) * PLACES + place - 2
                if 0 <= at < N_PIECES:
                    do(0, at)
            return between

        H_BANKS = (bank[4], bank[5])
        Y_BANKS = (bank[0], bank[1], bank[2], bank[3])
        X_BANKS, SLOT_BANK = (bank[6], bank[7]), bank[7]
        LAG = 2
        AHEAD = 3

        def hidden_pe(pe, e, b, f, inside=None):
            n = e * 2 * KF + b * KF + f
            if f == 0:
                pe.wait_ge(x_split, (e * 2 + b + 1) * NC)
            if b == 0:
                pe.wait_ge(w1_low, e * KF + f + 1)
            wait(pe, h_act, n - 1)
            for k in range(KD):
                for wpart, xpart in ((w1h, xTh), (w1h, xTl), (w1l, xTh)):
                    last = pe.matmul(H_BANKS[f % 2][:, :], wpart[:, f, k, :], xpart[:, b, k, :],
                                     start=(k == 0 and wpart is w1h and xpart is xTh),
                                     stop=(k == KD - 1 and wpart is w1l))
                if k == 1 and inside is not None:
                    choice_pe(pe, 1, inside)
            last.then_inc(h_sum, 1)

        def output_pe(pe, e, b, f, inside=None):
            n = e * 2 * KF + b * KF + f
            pe.wait_ge(h_split, n + 1)
            if b == 0:
                pe.wait_ge(w2_low, e * KF + f + 1)
            if f == 0:
                wait(pe, y_act, (e * 2 + b) * 2)
                wait(pe, y_dve, (e * 2 + b) * 2)
            for c in range(NC):
                for hpart, wpart in ((hh, w2h), (hh, w2l), (hl, w2h)):
                    last = pe.matmul(Y_BANKS[c][:, :], hpart[:, f % 2, c * P:(c + 1) * P], wpart[:, f, :],
                                     start=(f == 0 and hpart is hh and wpart is w2h),
                                     stop=(f == KF - 1 and hpart is hl))
                if c == 0 and inside is not None:
                    choice_pe(pe, 1, inside)
            last.then_inc(y_sum, 1)

        def slots_pe(pe, g):
            pe.wait_ge(hot, g + 1)
            for t in range(TB):
                last = pe.matmul(SLOT_BANK[:, 0:NC * NV], onehot[:, t, :],
                                 carried[:, t, :, :].rearrange("p c v -> p (c v)"),
                                 start=(t == 0), stop=(t == TB - 1))
            last.then_inc(slots_sum, 1)

        def tokens_pe(pe, g, c):
            pe.wait_ge(gathered[c], (g + 1) * 16)
            wait(pe, x_split, g * NC + c - 1)
            for k in range(KD):
                last = pe.transpose(X_BANKS[c % 2][:, k * P:(k + 1) * P], xg[:, c, k * P:(k + 1) * P], ident[:, :])
            last.then_inc(x_turned, 1)

        def hot_dve(dve, g, e, b):
            wait(dve, slots_sum, g)
            lo = slot_lo[:, b, :, bass.ds(e, 1)] if not isinstance(e, int) else slot_lo[:, b, :, e:e + 1]
            hi = slot_hi[:, b, :, bass.ds(e, 1)] if not isinstance(e, int) else slot_hi[:, b, :, e:e + 1]
            va = values[:, b, :, bass.ds(e, 1), :] if not isinstance(e, int) else values[:, b, :, e:e + 1, :]
            dve.tensor_tensor(onehot[:, :, :], iota_slot[:, :].unsqueeze(1).to_broadcast([P, TB, P]),
                              lo.to_broadcast([P, TB, P]), ALU.is_equal)
            dve.tensor_tensor(blockhot[:, :, :], iota_block[:, :].unsqueeze(1).to_broadcast([P, TB, NC]),
                              hi.to_broadcast([P, TB, NC]), ALU.is_equal).then_inc(slots_own, 1)
            dve.wait_ge(slots_own, g * 4 + 1)
            dve.tensor_tensor(carried[:, :, :, :], blockhot[:, :, :].unsqueeze(3).to_broadcast([P, TB, NC, NV]),
                              va.to_broadcast([P, TB, NC, NV]), ALU.mult).then_inc(hot, 1)

        def slots_dve(dve, g, b):
            dve.wait_ge(slots_sum, g + 1)
            dve.tensor_copy(got[:, :, :], SLOT_BANK[:, 0:NC * NV].rearrange("p (c v) -> p c v", c=NC))\
               .then_inc(slots_own, 1)
            dve.wait_ge(slots_own, g * 4 + 2)
            dve.tensor_tensor(slot_gate[:, b, 0, :], got[:, :, 3], got[:, :, 4], ALU.add).then_inc(slots_own, 1)
            dve.wait_ge(slots_own, g * 4 + 3)
            dve.tensor_tensor(slot_gate[:, b, 1, :], got[:, :, 2], slot_gate[:, b, 0, :], ALU.add)\
               .then_inc(slots_own, 1)
            for c in range(NC):
                wait(dve, scattered[c], (g - 1) * 16)
            dve.scalar_tensor_tensor(out=slot_row[:, b, :], in0=got[:, :, 0], scalar=float(P), in1=got[:, :, 1],
                                     op0=ALU.mult, op1=ALU.add).then_inc(slots_ready, 1)

        def split_tokens_dve(dve, g, b, c):
            dve.wait_ge(x_turned, g * NC + c + 1)
            src = X_BANKS[c % 2][:, :].rearrange("p (k t) -> p k t", k=KD)
            high, low = xTh[:, b, :, c * P:(c + 1) * P], xTl[:, b, :, c * P:(c + 1) * P]
            dve.tensor_copy(high, src).then_inc(x_high, 1)
            dve.wait_ge(x_high, g * NC + c + 1)
            dve.tensor_tensor(low, src, high.bitcast(F32), ALU.subtract).then_inc(x_split, 1)

        def split_hidden_dve(dve, e, b, f):
            n = e * 2 * KF + b * KF + f
            dve.wait_ge(h_act, n + 1)
            wait(dve, y_sum, n - 1)
            dve.tensor_copy(hh[:, f % 2, :], hf[:, f % 2, :]).then_inc(h_high, 1)
            dve.wait_ge(h_high, n + 1)
            dve.tensor_tensor(hl[:, f % 2, :], hf[:, f % 2, :], hh[:, f % 2, :].bitcast(F32), ALU.subtract)\
               .then_inc(h_split, 1)

        def gelu_act(act, e, b, f):
            n = e * 2 * KF + b * KF + f
            act.wait_ge(h_sum, n + 1)
            wait(act, h_split, n - 1)
            act.activation(hf[:, f % 2, :], H_BANKS[f % 2][:, :], ACT.Gelu).then_inc(h_act, 1)

        def output_rows(eng, e, b, c, done):
            g = e * 2 + b
            eng.wait_ge(y_sum, e * 2 * KF + (b + 1) * KF)
            wait(eng, scattered[c], g * 16)
            gate = slot_gate[:, b, 1, c:c + 1]
            if eng is nc.scalar:
                ins = eng.activation(y[:, c, :], Y_BANKS[c][:, :], ACT.Copy, scale=gate)
            else:
                ins = eng.tensor_scalar(y[:, c, :], Y_BANKS[c][:, :], gate, None, ALU.mult)
            ins.then_inc(done, 1)

        def weight_high_act(act, e, f):
            n = e * KF + f
            used = (e - 1) * 2 * KF + KF + f + 1
            wait(act, h_sum, used)
            wait(act, y_sum, used)
            act.wait_ge(w1_in[f % 2], e * (KF // 2) * 16 + (f // 2 + 1) * 16)
            act.activation(w1h[:, f, :, :], raw1[:, f % 2, :, :], ACT.Copy).then_inc(w1_high, 1)
            act.wait_ge(w2_in[f % 2], e * (KF // 2) * 16 + (f // 2 + 1) * 16)
            act.activation(w2h[:, f, :], raw2[:, f % 2, :], ACT.Copy).then_inc(w2_high, 1)

        def weight_low_pool(pool, e, f):
            n = e * KF + f
            pool.wait_ge(w1_high, n + 1)
            pool.tensor_tensor(w1l[:, f, :, :], raw1[:, f % 2, :, :], w1h[:, f, :, :].bitcast(F32), ALU.subtract)\
                .then_inc(w1_low, 1)
            pool.wait_ge(w2_high, n + 1)
            pool.tensor_tensor(w2l[:, f, :], raw2[:, f % 2, :], w2h[:, f, :].bitcast(F32), ALU.subtract)\
                .then_inc(w2_low, 1)

        def gather_pool(pool, g, b, c):
            pool.wait_ge(slots_ready, g + 1)
            wait(pool, x_turned, (g - 1) * NC + c + 1)
            pool.sem_inc(gathers, 1)
            pool.indirect_dma_start(xg[:, c, :], None, xn_rows,
                                    bass.IndirectOffsetOnAxis(ap=slot_row[:, b, c:c + 1], axis=0))\
                .then_inc(gathered[c], 16)

        def scatter_pool(pool, e, b, c):
            g = e * 2 + b
            done, at = (y_act, c) if c < 2 else (y_dve, c - 2)
            pool.wait_ge(done, g * 2 + at + 1)
            for other in range(NC):
                wait(pool, scattered[other], g * 16)
            pool.sem_inc(scatters, 1)
            pool.indirect_dma_start(out_rows, bass.IndirectOffsetOnAxis(ap=slot_row[:, b, c:c + 1], axis=0),
                                    y[:, c, :], None, compute_op=ALU.add).then_inc(scattered[c], 16)

        USUAL = (1, 3, (4, 6, 8, 10), (6, 8, 10, 12))
        FIRST = (9, 10, (10, 11, 12, 13), (12, 13, 14, 15))
        CHOICE_PER_STEP = 2

        def next_group(e, b):
            return (e, 1) if b == 0 else (e + 1, 0)

        def plan(e, b):
            return FIRST if isinstance(e, int) and e == 0 and b == 0 else USUAL

        def choice_pieces(e, b, f):
            if isinstance(e, int) and e == 0 and b == 0 and f >= 0:
                first = 1 + f * CHOICE_PER_STEP
                return [n for n in range(first, first + CHOICE_PER_STEP) if n < N_PIECES]
            return []

        def new_weights(e, b, f, final):
            if isinstance(e, int) and e == 0 and b == 0:
                return [(0, f + AHEAD)] if f + AHEAD < KF else []
            if b == 0 and f < LAG and not (isinstance(e, int) and e == 0):
                return [(e, KF - LAG + f)]
            if b == 1 and f >= LAG and not final:
                return [(e + 1, f - LAG)]
            return []

        def expert_pe(pe, e, final):
            for b in range(B):
                end = final and b == B - 1
                ne, nb = next_group(e, b)
                g = e * 2 + b + 1
                hot_at, slots_at, gather_at, turn_at_f = plan(e, b)
                for f in range(KF):
                    late, soon = (choice_pieces(e, b, f - 1) + [None, None])[1], (choice_pieces(e, b, f) + [None])[0]
                    if f + 1 < KF:
                        hidden_pe(pe, e, b, f + 1, late)
                    if not end and f == slots_at:
                        slots_pe(pe, g)
                    for c in range(NC):
                        if not end and turn_at_f[c] == f:
                            tokens_pe(pe, g, c)
                    if f + 1 == KF and not end:
                        hidden_pe(pe, ne, nb, 0)
                    output_pe(pe, e, b, f, soon)

        def expert_dve(dve, own, e, final):
            for b in range(B):
                end = final and b == B - 1
                ne, nb = next_group(e, b)
                g = e * 2 + b + 1
                hot_at, slots_at, gather_at, turn_at_f = plan(e, b)
                for f in range(KF):
                    for piece in choice_pieces(e, b, f)[:1]:
                        choice_dve(dve, own, 1, piece)
                    if f + 1 < KF:
                        split_hidden_dve(dve, e, b, f + 1)
                    for piece in choice_pieces(e, b, f)[1:]:
                        choice_dve(dve, own, 1, piece)
                    if not end:
                        if f == hot_at:
                            hot_dve(dve, g, ne, nb)
                        if f == slots_at:
                            slots_dve(dve, g, nb)
                        for c in range(NC):
                            if turn_at_f[c] == f:
                                split_tokens_dve(dve, g, nb, c)
                    if f + 1 == KF and not end:
                        split_hidden_dve(dve, ne, nb, 0)
                for c in (2, 3):
                    output_rows(dve, e, b, c, y_dve)

        def expert_act(act, e, final):
            for b in range(B):
                end = final and b == B - 1
                ne, nb = next_group(e, b)
                for f in range(KF):
                    if f + 1 < KF:
                        gelu_act(act, e, b, f + 1)
                    elif not end:
                        gelu_act(act, ne, nb, 0)
                    for chunk in new_weights(e, b, f, final):
                        weight_high_act(act, *chunk)
                for c in (0, 1):
                    output_rows(act, e, b, c, y_act)

        def expert_pool(pool, e, final):
            for b in range(B):
                end = final and b == B - 1
                ne, nb = next_group(e, b)
                g = e * 2 + b + 1
                hot_at, slots_at, gather_at, turn_at_f = plan(e, b)
                for f in range(KF):
                    for chunk in new_weights(e, b, f, final):
                        weight_low_pool(pool, *chunk)
                    for c in range(NC):
                        if not end and gather_at[c] == f:
                            gather_pool(pool, g, nb, c)
                for c in range(NC):
                    scatter_pool(pool, e, b, c)

        def load_weights(sp, e, f):
            n = e * KF + f
            wait(sp, w1_low, n - 1)
            sp.dma_start(raw1[:, f % 2, :, :], w1_v[e, :, :, f * P:(f + 1) * P] if isinstance(e, int) else
                         w1_v[bass.ds(e, 1), :, :, f * P:(f + 1) * P].rearrange("o p k f -> (o p) k f"))\
              .then_inc(w1_in[f % 2], 16)
            wait(sp, w2_low, n - 1)
            sp.dma_start(raw2[:, f % 2, :], w2_v[e, :, f, :] if isinstance(e, int) else
                         w2_v[bass.ds(e, 1), :, f, :].rearrange("o p d -> (o p) d"))\
              .then_inc(w2_in[f % 2], 16)

        CONSTS = 8

        @block.sync
        def _(sp):
            small = [(bias_rows[0:KD, :], bk.rearrange("(c p) -> c p", p=P)),
                     (bias_rows[KD:2 * KD, :], bv.rearrange("(c p) -> c p", p=P)),
                     (bias_rows[2 * KD:3 * KD, :], bq.rearrange("(c p) -> c p", p=P)),
                     (bo_all[:, :], bo.rearrange("(a d) -> a d", a=1).to_broadcast([J, D])),
                     (gate_raw[:, :], gate_w)]
            sp.dma_start(raw_k[:, :, :], Wk.rearrange("(c p) e -> p c e", p=P)).then_inc(lin[2], 16)
            for dst, src in small:
                sp.dma_start(dst, src).then_inc(lin[0], 16)
            sp.dma_start(ctx_raw[:, :, :], ctx_in.rearrange("b j d -> j b d")).then_inc(lin[1], 16)
            sp.dma_start(x_s[:, 0, :, :], x_q[0]).then_inc(x_in[0], 16)
            sp.dma_start(raw_q[:, :, :], Wq.rearrange("(c p) e -> p c e", p=P)).then_inc(lin[3], 16)
            sp.dma_start(raw_v[:, :, :], Wv.rearrange("(c p) e -> p c e", p=P)).then_inc(lin[4], 16)
            sp.dma_start(x_s[:, 1, :, :], x_q[1]).then_inc(x_in[1], 16)
            sp.dma_start(raw_o[:, :, :], Wo.rearrange("(c p) e -> p c e", p=P)).then_inc(lin[5], 16)
            sp.dma_start(mask_i[:, :, :], mask_v).then_inc(mask_in, 16)
            sp.dma_start(x_s[:, 2, :, :], x_q[2]).then_inc(x_in[2], 16)
            for q in range(NQ):
                sp.wait_ge(added, Q * q + Q)
                sp.dma_start(out_q[q], x1[:, q % 2, :, :]).then_inc(x1_out[q % 2], 16)
                if q + 3 < NQ:
                    sp.dma_start(x_s[:, q % 3, :, :], x_q[q + 3]).then_inc(x_in[q % 3], 16)
                sp.wait_ge(normed2, Q * q + Q)
                sp.dma_start(xn_q[q], xn2[:, q % 2, :, :]).then_inc(xn_out[q % 2], 16)
            sp.wait_ge(logit_out, NQ)
            rows_stored(sp)
            for f in range(KF):
                load_weights(sp, 0, f)
            with sp.Fori(1, E) as e:
                for f in range(KF):
                    load_weights(sp, e, f)
            for c in range(NC):
                sp.wait_ge(scattered[c], 16 * G)

        @block.gpsimd
        def _(pool):
            pool.dma_start(gates_raw[:, 0:1], g_xattn.rearrange("(a o) -> a o", o=1).to_broadcast([P, 1]))\
                .then_inc(lin[6], 16)
            pool.dma_start(gates_raw[:, 1:2], g_ffn.rearrange("(a o) -> a o", o=1).to_broadcast([P, 1]))\
                .then_inc(lin[6], 16)
            pool.memset(ident[:, :], 0.0).then_inc(pool_start, 1)
            pool.memset(powers[:, :], -0.5).then_inc(pool_start, 1)
            pool.memset(vo[:, :, :], 0.0).then_inc(pool_start, 1)
            pool.memset(vg[:, :, :], 0.0).then_inc(pool_start, 1)
            pool.wait_ge(pool_start, 1)
            pool.affine_select(out=ident[:, :], in_=ident[:, :], compare_op=ALU.not_equal, fill=1.0, base=0,
                               pattern=[[-1, P]], channel_multiplier=1).then_inc(consts, 1)
            pool.memset(mean_m[:, :], 1.0 / D).then_inc(consts, 1)
            pool.wait_ge(pool_start, 4)
            pool.memset(eT[:, :, :], 0.0).then_inc(consts, 1)
            pool.memset(ones_m[:, :], 1.0).then_inc(consts, 1)
            pool.memset(below_m[:, :], 1.0).then_inc(pool_start, 1)
            for c in range(3):
                pool.memset(bit_table[:, 0, c, :], (c + 1) << (BITS - 2)).then_inc(consts, 1)
            pool.wait_ge(pool_start, 5)
            pool.affine_select(out=below_m[:, :], in_=below_m[:, :], compare_op=ALU.is_gt, fill=0.0, base=0,
                               pattern=[[1, P]], channel_multiplier=-1).then_inc(consts, 1)
            pool.iota(vrow_i[:, :], pattern=[[1, NT]], base=0, channel_multiplier=0).then_inc(iotas, 1)
            pool.iota(vpar_i[:, :], pattern=[[1, 1]], base=0, channel_multiplier=1).then_inc(iotas, 1)
            pool.iota(iota_i[:, :], pattern=[[1, P]], base=0, channel_multiplier=0).then_inc(iotas, 1)
            attention_pool(pool)
            rows_stored(pool)
            for c in range(NC):
                gather_pool(pool, 0, 0, c)
            for f in range(AHEAD):
                weight_low_pool(pool, 0, f)
            expert_pool(pool, 0, False)
            with pool.Fori(1, E - 1) as e:
                expert_pool(pool, e, False)
            expert_pool(pool, E - 1, True)

        @block.scalar
        def _(act):
            act.wait_ge(lin[6], 32)
            act.activation(gates[:, :], gates_raw[:, :], ACT.Tanh).then_inc(gates_done, 1)
            prep_out(act, prep_act, True)
            attention_act(act)
            for f in range(AHEAD):
                if f == 2:
                    choice_act(act, 1)
                    act.activation(spare_gate[:, :], gates[:, 0:1], ACT.Gelu)
                weight_high_act(act, 0, f)
            gelu_act(act, 0, 0, 0)
            expert_act(act, 0, False)
            with act.Fori(1, E - 1) as e:
                expert_act(act, e, False)
            expert_act(act, E - 1, True)

        @block.vector
        def _(dve):
            own = Tally(dve_own)
            prep_out(dve, prep_dve, False)
            dve.wait_ge(iotas, 3)
            for b in range(B):
                own.mark(dve.tensor_copy(values[:, b, :, :, 0],
                                         vrow_i[:, b * TB:(b + 1) * TB].unsqueeze(2).to_broadcast([P, TB, E])))
                own.mark(dve.tensor_copy(values[:, b, :, :, 1],
                                         vpar_i[:, 0:1].unsqueeze(2).to_broadcast([P, TB, E])))
            own.mark(dve.tensor_copy(iota_slot[:, :], iota_i[:, :]))
            own.mark(dve.tensor_scalar(iota_block[:, :], iota_i[:, 0:NC], 1.0, None, ALU.add))
            dve.wait_ge(consts, CONSTS)
            for s in range(1, STEPS):
                own.mark(dve.tensor_scalar(bit_table[:, s, :, :], bit_table[:, 0, :, :], 2 * s, None,
                                           ALU.logical_shift_right))
            attention_dve(dve, own, beside_attention(lambda b, n: choice_dve(dve, own, b, n)))
            dve.wait_ge(logit_out, NQ)
            rows_stored(dve)
            hot_dve(dve, 0, 0, 0)
            slots_dve(dve, 0, 0)
            choice_dve(dve, own, 1, 0)
            for c in range(NC):
                split_tokens_dve(dve, 0, 0, c)
            split_hidden_dve(dve, 0, 0, 0)
            expert_dve(dve, own, 0, False)
            with dve.Fori(1, E - 1) as e:
                expert_dve(dve, None, e, False)
            expert_dve(dve, None, E - 1, True)

        @block.tensor
        def _(pe):
            prep_pe(pe)
            attention_pe(pe, beside_attention(lambda b, n: choice_pe(pe, b, n)))
            slots_pe(pe, 0)
            for c in range(NC):
                tokens_pe(pe, 0, c)
            hidden_pe(pe, 0, 0, 0, 0)
            expert_pe(pe, 0, False)
            with pe.Fori(1, E - 1) as e:
                expert_pe(pe, e, False)
            expert_pe(pe, E - 1, True)


INPUTS = ["x", "ctx_1024", "mask_BxSxS2_ik0", "g_xattn", "g_ffn", "L0_xattn_Wq", "L0_xattn_bq", "L0_xattn_Wk",
          "L0_xattn_bk", "L0_xattn_Wv", "L0_xattn_bv", "L0_xattn_Wo", "L0_xattn_bo", "L0_ffn_gate_w", "L0_ffn_w1",
          "L0_ffn_w2"]


def kernel(**inputs):
    import concourse.bacc as bacc
    from concourse.bass_utils import run_bass_kernel_spmd

    nc = bacc.Bacc("TRN2", target_bir_lowering=False, num_devices=1)
    arrays, args = {}, []
    for name in INPUTS:
        a = np.ascontiguousarray(inputs[name])
        arrays[f"in_{name}"] = a
        args.append(nc.dram_tensor(f"in_{name}", a.shape, mybir.dt.from_np(a.dtype), kind="ExternalInput").ap())
    shape = inputs["x"].shape
    args.append(nc.dram_tensor("layer_out", shape, F32, kind="ExternalOutput").ap())
    flamingo_layer(nc, *args)
    r = run_bass_kernel_spmd(nc, [arrays], core_ids=[0])
    return r.results[0]["layer_out"]
```

```python
from contextlib import ExitStack

import numpy as np

import concourse.bass as bass
from concourse import mybir

F32 = mybir.dt.float32
F32R = mybir.dt.float32r
BF16 = mybir.dt.bfloat16
I32 = mybir.dt.int32
U32 = mybir.dt.uint32
ALU = mybir.AluOpType
ACT = mybir.ActivationFunctionType
AX = mybir.AxisListType

P = 128
BANK = 512
EPS = 1e-5
MASKED = -1.0e30
BITS = 30
BITS_PER_STEP = 3
CANDS = 2 ** BITS_PER_STEP - 1
STEPS = BITS // BITS_PER_STEP


def wait(eng, sem, value):
    if not isinstance(value, int) or value > 0:
        eng.wait_ge(sem, value)


class Tally:

    def __init__(self, sem):
        self.sem, self.n = sem, 0

    def mark(self, ins):
        ins.then_inc(self.sem, 1)
        self.n += 1
        return self.n


def flamingo_layer(nc, x, ctx_in, mask, g_xattn, g_ffn, Wq, bq, Wk, bk, Wv, bv, Wo, bo, gate_w, w1, w2, out):
    B, S, D = x.shape
    J = ctx_in.shape[1]
    E, _, F = w1.shape
    CAP = 2 * S // E
    KD = D // P
    KF = F // P
    TB = S // P
    NT = B * TB
    Q = 4
    NQ = NT // Q
    QB = NQ // B
    NC = CAP // P
    G = B * E
    BJ = B * J
    JE = J + E
    NV = 5
    SCALE = float(D) ** -0.5
    assert JE <= P and D == BANK and CAP == BANK and J <= P and KD == NC == 4 and KF == 16 and B == 2 and E == 8

    x_q = x.rearrange("b (q i p) d -> (b q) p i d", i=Q, p=P)
    out_rows = out.rearrange("b s d -> (b s) d")
    out_q = out_rows.rearrange("(q i p) d -> q p i d", i=Q, p=P)
    xn_rows = [nc.dram_tensor(f"xn_rows{b}", [S, D], F32, kind="Internal").ap() for b in range(B)]
    xn_q = [t.rearrange("(q i p) d -> q p i d", i=Q, p=P) for t in xn_rows]
    mask_v = mask.rearrange("b (t p) j -> p (b t) j", p=P)
    w1_v = w1.rearrange("e (k p) f -> e p k f", p=P)
    w2_v = w2.rearrange("e (c p) d -> e p c d", p=P)

    whole = ExitStack()
    with whole:
        def sem(name):
            return whole.enter_context(nc.semaphore(name))

        def keep(name, shape, dt):
            return whole.enter_context(nc.sbuf_tensor(name, shape, dt))

        bank = [whole.enter_context(nc.psum_tensor(f"bank{i}", [P, BANK], F32)) for i in range(8)]

        ident = keep("ident", [P, P], F32)
        iota_slot = keep("iota_slot", [P, P], BF16)
        iota_block = keep("iota_block", [P, NC], BF16)
        slot_lo = keep("slot_lo", [P, B, TB, E], BF16)
        slot_hi = keep("slot_hi", [P, B, TB, E], BF16)
        values = keep("values", [P, B, TB, E, NV], BF16)
        gates = keep("gates", [P, 2], F32)
        logits = keep("logits", [P, B, TB, E], F32)

        chooser = ExitStack()

        def choice(name, dt, shape=(P, TB, E)):
            return chooser.enter_context(nc.sbuf_tensor(name, list(shape), dt))

        with chooser:
            prob = choice("prob", F32)
            pexp = choice("pexp", F32)
            pstat = choice("pstat", F32, (P, 3, TB))
            ones_m = choice("ones_m", BF16, (P, P))
            below_m = choice("below_m", BF16, (P, P))
            bit_table = choice("bit_table", I32, (P, STEPS, CANDS, 1))
            cand = choice("cand", I32, (P, CANDS, E))
            found = choice("found", F32, (P, 2, CANDS + 1, E))
            atleast = choice("atleast", BF16, (P, CANDS, TB, E))
            count = choice("count", BF16, (P, CANDS, E))
            above = choice("above", BF16)
            tied = choice("tied", BF16)
            need = choice("need", F32, (P, E))
            chosen = choice("chosen", BF16)
            fits = choice("fits", BF16)
            tied_taken = choice("tied_taken", F32)
            place_i = choice("place_i", I32)
            block_i = choice("block_i", I32)
            part_i = choice("part_i", I32)
        y = keep("y", [P, NC, D], F32)

        onehot = keep("onehot", [P, TB, P], BF16)
        blockhot = keep("blockhot", [P, TB, NC], BF16)
        carried = keep("carried", [P, TB, NC, NV], BF16)
        got = keep("got", [P, NC, NV], F32)
        slot_gate = keep("slot_gate", [P, B, 2, NC], F32)
        slot_row = keep("slot_row", [P, B, NC], U32)
        slot_source = keep("slot_source", [P, NC], U32)
        spare_gate = keep("spare_gate", [P, 1], F32)
        xg = keep("xg", [P, NC, D], F32)
        xTh = keep("xTh", [P, B, KD, CAP], F32R)
        xTl = keep("xTl", [P, B, KD, CAP], F32R)

        early = ExitStack()

        def first(name, shape, dt, stack=early):
            return stack.enter_context(nc.sbuf_tensor(name, shape, dt))

        with early:
            mean_m = first("mean_m", [P, P], F32)
            bias_rows = first("bias_rows", [3 * KD, P], F32)
            bo_all = first("bo_all", [J, D], F32)
            gate_raw = first("gate_raw", [E, D], F32)
            cols = first("cols", [P, 3 * KD + KD * E], F32)
            ctx_raw = first("ctx_raw", [J, B, D], F32)
            ctxT = first("ctxT", [P, KD, B, J], F32)
            kT = first("kT", [P, KD, BJ], F32)
            vT = first("vT", [P, KD, BJ], F32)
            qkg = first("qkg", [P, KD, B, JE], F32)
            voT = first("voT", [P, KD, B, J], F32)
            projections = ExitStack()
            with projections:
                raw_k, raw_q, raw_v, raw_o, wkT, wvT, woT = (
                    first(n, [P, KD, D], F32, projections)
                    for n in ("raw_k", "raw_q", "raw_v", "raw_o", "wkT", "wvT", "woT"))
            xT = first("xT", [P, 2, KD, Q * P], F32)
            sT = first("sT", [JE, 2, Q * P], F32)
            x1 = first("x1", [P, 2, Q, D], F32)
            xn2 = first("xn2", [P, 2, Q, D], F32)
            sc = first("sc", [P, 2, Q, J], F32)
            ex = first("ex", [P, 2, Q, J], F32)
            gates_raw = first("gates_raw", [P, 2], F32)
            qkc = first("qkc", [P, KD, B, JE], F32)
            cb = first("cb", [P, B, J], F32)
            vo = first("vo", [P, B, D], F32)
            vg = first("vg", [P, B, E], F32)
            mask_i = first("mask_i", [P, NT, J], I32)
            mflag = first("mflag", [P, Q, J], F32)
            mbias = first("mbias", [P, 2, Q, J], F32)
            eT = first("eT", [P, 2, Q * P], F32)
            spare = first("spare", [P, Q, D], BF16)
            xsum = first("xsum", [P, 2, Q], F32)
            xmean = first("xmean", [P, 2, Q], F32)
            xvar = first("xvar", [P, 2, Q], F32)
            st2 = first("st2", [P, Q, 6], F32)
            mv2 = first("mv2", [P, 2, Q, 2], F32)
            norm1 = first("norm1", [P, 2, 2, Q], F32)
            norm2 = first("norm2", [P, 2, 4, Q], F32)
            powers = first("powers", [P, Q], F32)
            smax = first("smax", [P, 2, Q], F32)
            smaxn = first("smaxn", [P, 2, Q], F32)
            rsum = first("rsum", [P, 2, Q], F32)
            rinv = first("rinv", [P, 2, Q], F32)
            xg1 = first("xg1", [P, 2, Q, E], F32)
            lg1 = first("lg1", [P, 2, Q, E], F32)
            vrow_i = first("vrow_i", [P, NT], I32)
            vpar_i = first("vpar_i", [P, 1], I32)
            iota_i = first("iota_i", [P, P], I32)
            x_s = first("x_s", [P, 3, Q, D], F32)

        weights = keep("weights", [P, KF, 4, D], F32R)
        W1_HIGH, W1_LOW, W2_HIGH, W2_LOW = range(4)
        hf = keep("hf", [P, 2, CAP], F32)
        hh = keep("hh", [P, 2, CAP], F32R)
        hl = keep("hl", [P, 2, CAP], F32R)
        raw1 = keep("raw1", [P, 2, KD, P], F32)
        raw2 = keep("raw2", [P, 2, D], F32)

        consts = sem("consts")
        pool_start = sem("pool_start")
        lin = [sem(f"lin{i}") for i in range(7)]
        prep_full = sem("prep_full")
        prep_act = sem("prep_act")
        prep_dve = sem("prep_dve")
        gates_done = sem("gates_done")
        vo_sum = sem("vo_sum")
        x_in = [sem(f"x_in{i}") for i in range(3)]
        mask_in = sem("mask_in")
        x_summed = sem("x_summed")
        mean_ready = sem("mean_ready")
        squares_done = sem("squares_done")
        x1_stats = sem("x1_stats")
        pool_own = sem("pool_own")
        dve_own = sem("dve_own")
        normed1 = sem("normed1")
        deviated2 = sem("deviated2")
        normed2 = sem("normed2")
        turned = sem("turned")
        turn_out = sem("turn_out")
        scored = sem("scored")
        mask_ready = sem("mask_ready")
        sc_ready = sem("sc_ready")
        smax_ready = sem("smax_ready")
        exped = sem("exped")
        weighed = sem("weighed")
        routed = sem("routed")
        added = sem("added")
        logit_out = sem("logit_out")
        x1_out = [sem(f"x1_out{i}") for i in range(2)]
        xn_out = [sem(f"xn_out{i}") for i in range(2)]

        pdiff = sem("pdiff")
        pexped = sem("pexped")
        bit_count = sem("bit_count")
        bit_total = sem("bit_total")
        pick_in = sem("pick_in")
        pick_sum = sem("pick_sum")
        iotas = sem("iotas")

        w1_in = [sem(f"w1_in{i}") for i in range(2)]
        w2_in = [sem(f"w2_in{i}") for i in range(2)]
        w1_high = sem("w1_high")
        w2_high = sem("w2_high")
        w1_low = sem("w1_low")
        w2_low = sem("w2_low")
        hot = sem("hot")
        slots_sum = sem("slots_sum")
        slots_own = sem("slots_own")
        row_ready = sem("row_ready")
        slots_ready = sem("slots_ready")
        gathered = [sem(f"gathered{i}") for i in range(NC)]
        gathers = sem("gathers")
        scatters = sem("scatters")
        x_turned = sem("x_turned")
        x_high = sem("x_high")
        x_split = sem("x_split")
        h_sum = sem("h_sum")
        h_act = sem("h_act")
        h_high = sem("h_high")
        h_split = sem("h_split")
        y_sum = sem("y_sum")
        y_chunk = sem("y_chunk")
        y_act = sem("y_act")
        y_dve = sem("y_dve")
        scattered = [sem(f"scattered{i}") for i in range(NC)]

        block = whole.enter_context(nc.Block())

        steps = []

        def add(name, i, by, after=None):
            steps.append((name, i, by, None if after is None else step_at[after]))
            step_at[name, i] = len(steps) - 1

        step_at = {}
        by_turns = ["act", "dve"]
        add("cols", 0, "act")
        for b in range(B):
            add("ctx", b, by_turns[(b + 1) % 2])
        for k in range(KD):
            add("turn_k", k, by_turns[(k + 1) % 2])
        for h in range(2):
            add("kT", h, by_turns[(h + 1) % 2], ("turn_k", KD - 1))
        add("turn_v", 0, "dve")
        for h in range(2):
            add("qk", h, by_turns[h], ("kT", 1))
        add("cb", 0, "act", ("kT", 1))
        add("turn_v", 1, "dve")
        add("turn_v", 2, "act")
        add("mean", 0, "dve", ("qk", 1))
        add("turn_v", 3, "act")
        add("turn_o", 0, "act")
        add("turn_o", 1, "dve")
        for h in range(2):
            add("vT", h, by_turns[h], ("turn_v", 3))
        for k in range(2, KD):
            add("turn_o", k, by_turns[k % 2])
        for b in range(B):
            add("vo", b, "dve", ("turn_o", KD - 1))
        for b in range(B):
            add("voT", b, "act", ("vo", b))
        add("vg", 0, "dve", ("voT", B - 1))
        PREP_BANKS = (bank[0], bank[1], bank[5], bank[7])
        BC = 3 * KD
        needs_in = {"cols": (0, 5 * 16), "ctx": (1, 16), "turn_k": (2, 16), "qk": (3, 16), "turn_v": (4, 16),
                    "turn_o": (5, 16)}

        def wait_evacuated(eng, n):
            for by, done in (("act", prep_act), ("dve", prep_dve)):
                wait(eng, done, sum(step[2] == by for step in steps[:n + 1]))

        def prep_pe(pe):
            pe.wait_ge(consts, 1)
            for n, (name, i, _, after) in enumerate(steps):
                bk = PREP_BANKS[n % 4]
                if name in needs_in:
                    which, value = needs_in[name]
                    pe.wait_ge(lin[which], value)
                if n >= 4:
                    wait_evacuated(pe, n - 4)
                if after is not None:
                    wait_evacuated(pe, after)
                if name == "cols":
                    pe.transpose(bk[:, 0:BC], bias_rows[:, :], ident[0:BC, 0:BC])
                    for k in range(KD):
                        last = pe.transpose(bk[:, BC + k * E:BC + (k + 1) * E], gate_raw[:, k * P:(k + 1) * P],
                                            ident[0:E, 0:E])
                elif name == "ctx":
                    for k in range(KD):
                        last = pe.transpose(bk[:, k * J:(k + 1) * J], ctx_raw[:, i, k * P:(k + 1) * P],
                                            ident[0:J, 0:J])
                elif name.startswith("turn"):
                    raw_w = {"turn_k": raw_k, "turn_v": raw_v, "turn_o": raw_o}[name]
                    for c in range(KD):
                        last = pe.transpose(bk[:, c * P:(c + 1) * P], raw_w[:, c, i * P:(i + 1) * P], ident[:, :])
                elif name in ("kT", "vT"):
                    wt = wkT if name == "kT" else wvT
                    for h in range(2):
                        for k in range(KD):
                            c = 2 * i + h
                            last = pe.matmul(bk[:, h * BJ:(h + 1) * BJ], wt[:, k, c * P:(c + 1) * P],
                                             ctxT[:, k, :, :].rearrange("p b j -> p (b j)"),
                                             start=(k == 0), stop=(k == KD - 1))
                elif name == "cb":
                    for c in range(KD):
                        last = pe.matmul(bk[:, 0:BJ], cols[:, 2 * KD + c:2 * KD + c + 1].to_broadcast([P, P]),
                                         kT[:, c, :], start=(c == 0), stop=(c == KD - 1))
                elif name == "mean":
                    pe.wait_ge(consts, 2)
                    for d in range(KD):
                        last = pe.matmul(bk[:, 0:B * JE], mean_m[:, :], qkg[:, d, :, :].rearrange("p b j -> p (b j)"),
                                         start=(d == 0), stop=(d == KD - 1))
                elif name == "qk":
                    for h in range(2):
                        for c in range(KD):
                            d = 2 * i + h
                            last = pe.matmul(bk[:, h * BJ:(h + 1) * BJ], raw_q[:, c, d * P:(d + 1) * P], kT[:, c, :],
                                             start=(c == 0), stop=(c == KD - 1))
                elif name == "vo":
                    for c in range(KD):
                        last = pe.matmul(bk[0:J, :], vT[:, c, i * J:(i + 1) * J], woT[:, c, :], start=(c == 0),
                                         stop=(c == KD - 1))
                elif name == "voT":
                    for k in range(KD):
                        last = pe.transpose(bk[:, k * J:(k + 1) * J], vo[0:J, i, k * P:(k + 1) * P],
                                            ident[0:J, 0:J])
                elif name == "vg":
                    for b in range(B):
                        for k in range(KD):
                            last = pe.matmul(bk[0:J, b * E:(b + 1) * E], voT[:, k, b, :], qkc[:, k, b, J:JE],
                                             start=(k == 0), stop=(k == KD - 1))
                last.then_inc(prep_full, 1)

        def prep_out(eng, mine, is_act):
            def copy(dst, src, scale=None, bias=None):
                if is_act:
                    if bias is not None:
                        return eng.activation(dst, src, ACT.Identity, bias=bias)
                    return eng.activation(dst, src, ACT.Copy, scale=1.0 if scale is None else scale)
                if bias is not None:
                    return eng.tensor_scalar(dst, src, bias, None, ALU.add)
                if scale is not None:
                    return eng.tensor_scalar(dst, src, scale, None, ALU.mult)
                return eng.tensor_copy(dst, src)

            for n, (name, i, by, _) in enumerate(steps):
                if (by == "act") != is_act:
                    continue
                bk = PREP_BANKS[n % 4]
                eng.wait_ge(prep_full, n + 1)
                if name == "cols":
                    last = copy(cols[:, :], bk[:, 0:BC + KD * E])
                elif name == "ctx":
                    last = copy(ctxT[:, :, i, :], bk[:, 0:KD * J].rearrange("p (k j) -> p k j", k=KD))
                elif name == "turn_k":
                    last = copy(wkT[:, i, :], bk[:, :])
                elif name == "turn_v":
                    last = copy(wvT[:, i, :], bk[:, :])
                elif name == "turn_o":
                    last = copy(woT[:, i, :], bk[:, :])
                elif name in ("kT", "vT"):
                    eng.wait_ge(prep_act, 1)
                    for h in range(2):
                        c = 2 * i + h
                        at = c + (0 if name == "kT" else KD)
                        last = copy((kT if name == "kT" else vT)[:, c, :], bk[:, h * BJ:(h + 1) * BJ],
                                    bias=cols[:, at:at + 1])
                elif name == "cb":
                    last = copy(cb[:, :, :].rearrange("p b j -> p (b j)"), bk[:, 0:BJ], scale=SCALE)
                elif name == "qk":
                    for h in range(2):
                        last = copy(qkg[:, 2 * i + h, :, 0:J],
                                    bk[:, h * BJ:(h + 1) * BJ].rearrange("p (b j) -> p b j", b=B), scale=SCALE)
                    if i == 1:
                        eng.wait_ge(prep_act, 1)
                        for b in range(B):
                            last = copy(qkg[:, :, b, J:JE], cols[:, BC:BC + KD * E].rearrange("p (k e) -> p k e", k=KD))
                elif name == "mean":
                    wait_evacuated(eng, step_at["qk", 1])
                    last = eng.tensor_tensor(qkc[:, :, :, :].rearrange("p k b j -> p k (b j)"),
                                             qkg[:, :, :, :].rearrange("p k b j -> p k (b j)"),
                                             bk[:, 0:B * JE].unsqueeze(1).to_broadcast([P, KD, B * JE]), ALU.subtract)
                elif name == "vo":
                    eng.wait_ge(gates_done, 1)
                    eng.wait_ge(consts, 3)
                    eng.tensor_tensor(vo[0:J, i, :], bk[0:J, :], bo_all[:, :], ALU.add).then_inc(vo_sum, 1)
                    eng.wait_ge(vo_sum, i + 1)
                    last = eng.tensor_scalar(vo[0:J, i, :], vo[0:J, i, :], gates[0:J, 0:1], None, ALU.mult)
                elif name == "voT":
                    last = copy(voT[:, :, i, :], bk[:, 0:KD * J].rearrange("p (k j) -> p k j", k=KD))
                elif name == "vg":
                    last = copy(vg[0:J, :, :], bk[0:J, 0:B * E].rearrange("p (b e) -> p b e", b=B))
                last.then_inc(mine, 1)

        turns = []
        for it in range(NQ + 1):
            turns += [("x", it, i) for i in range(Q) if it < NQ]
            turns += [("e", it - 1, 0)] if it >= 1 else []
            turns += [("s", it, 0)] if it < NQ else []
        turn_at = {t: n for n, t in enumerate(turns)}
        T_BANKS = (2, 3, 4)
        O_BANKS = (bank[0], bank[1])
        VG_BANK, SC_BANK, CHOICE_BANK = bank[5], bank[6], bank[7]
        CHOOSE_FROM, PLACES = QB + 1, 3

        def turn_bank(turn):
            return bank[T_BANKS[turn_at[turn] % 3]]

        def pe_bank_free(pe, turn):
            wait(pe, turn_out, turn_at[turn] - 2)

        def attention_pe(pe, between):
            for it in range(NQ + 1):
                q = it
                if q < NQ:
                    pe.wait_ge(x_in[q % 3], 16 * (q // 3 + 1))
                    for i in range(Q):
                        pe_bank_free(pe, ("x", q, i))
                        for k in range(KD):
                            last = pe.transpose(turn_bank(("x", q, i))[:, k * P:(k + 1) * P],
                                                x_s[:, q % 3, i, k * P:(k + 1) * P], ident[:, :])
                        last.then_inc(turned, 1)
                between(it - 1, 1)
                q = it - 1
                if q >= 0:
                    pe.wait_ge(exped, q + 1)
                    pe_bank_free(pe, ("e", q, 0))
                    for i in range(Q):
                        last = pe.transpose(turn_bank(("e", q, 0))[0:J, i * P:(i + 1) * P], ex[:, q % 2, i, :],
                                            ident[:, :])
                    last.then_inc(turned, 1)
                q = it
                if q < NQ:
                    b = q // QB
                    if q == 0:
                        wait_evacuated(pe, step_at["mean", 0])
                    pe_bank_free(pe, ("s", q, 0))
                    pe.wait_ge(turn_out, turn_at["x", q, Q - 1] + 1)
                    for k in range(KD):
                        last = pe.matmul(turn_bank(("s", q, 0))[0:JE, :], qkc[:, k, b, :], xT[:, q % 2, k, :],
                                         start=(k == 0), stop=(k == KD - 1))
                        if k == 2:
                            between(it - 1, 2)
                    last.then_inc(turned, 1)
                else:
                    between(it - 1, 2)
                for i in range(Q):
                    q = it - 1
                    if q >= 0:
                        b = q // QB
                        if i == 0:
                            if q == 0:
                                wait_evacuated(pe, len(steps) - 1)
                            pe.wait_ge(turn_out, turn_at["e", q, 0] + 1)
                            wait(pe, logit_out, q)
                        n = Q * q + i
                        wait(pe, added, n - 1)
                        pe.matmul(O_BANKS[n % 2][:, :], eT[:, q % 2, i * P:(i + 1) * P], vo[:, b, :],
                                  start=True, stop=True).then_inc(weighed, 1)
                        last = pe.matmul(VG_BANK[:, i * E:(i + 1) * E], eT[:, q % 2, i * P:(i + 1) * P], vg[:, b, :],
                                         start=True, stop=True)
                        if i == Q - 1:
                            last.then_inc(routed, 1)
                    q = it
                    if i == 1 and q < NQ:
                        pe.wait_ge(turn_out, turn_at["s", q, 0] + 1)
                        wait(pe, sc_ready, q)
                        for t in range(Q):
                            last = pe.transpose(SC_BANK[:, t * JE:(t + 1) * JE], sT[:, q % 2, t * P:(t + 1) * P],
                                                ident[0:JE, 0:JE])
                        last.then_inc(scored, 1)
                    if i == 1:
                        between(it, 0)
            between(NQ, 1)

        def attention_act(act):
            def sums(q):
                act.wait_ge(x_in[q % 3], 16 * (q // 3 + 1))
                wait(act, squares_done, q)
                for i in range(Q):
                    last = act.activation(spare[:, i, :], x_s[:, q % 3, i, :], ACT.Copy,
                                          accum_out=xsum[:, q % 2, i:i + 1])
                last.then_inc(x_summed, 1)
                act.wait_ge(x_summed, q + 1)
                act.activation(xmean[:, q % 2, :], xsum[:, q % 2, :], ACT.Copy, scale=-1.0 / D).then_inc(mean_ready, 1)

            def squares(q):
                act.wait_ge(mean_ready, q + 1)
                wait(act, normed1, q - 1)
                for i in range(Q):
                    last = act.activation(spare[:, i, :], x_s[:, q % 3, i, :], ACT.Square,
                                          bias=xmean[:, q % 2, i:i + 1], accum_out=xvar[:, q % 2, i:i + 1])
                last.then_inc(squares_done, 1)

            sums(0)
            for it in range(NQ + 1):
                q = it
                if q < NQ:
                    for i in range(Q):
                        act.wait_ge(turned, turn_at["x", q, i] + 1)
                        if q >= 2:
                            act.wait_ge(turned, turn_at["s", q - 2, 0] + 1)
                        act.activation(xT[:, q % 2, :, i * P:(i + 1) * P],
                                       turn_bank(("x", q, i))[:, :].rearrange("p (k t) -> p k t", k=KD), ACT.Copy)\
                           .then_inc(turn_out, 1)
                q = it - 1
                if q >= 0:
                    act.wait_ge(turned, turn_at["e", q, 0] + 1)
                    wait(act, routed, q - 1)
                    act.wait_ge(consts, 3)
                    act.activation(eT[0:J, q % 2, :], turn_bank(("e", q, 0))[0:J, :], ACT.Copy).then_inc(turn_out, 1)
                if it == CHOOSE_FROM:
                    choice_act(act, 0)
                if it == NQ:
                    for f in range(2):
                        weight_high_act(act, 0, f)
                q = it
                if q < NQ:
                    squares(q)
                    act.wait_ge(turned, turn_at["s", q, 0] + 1)
                    wait(act, scored, q - 1)
                    act.activation(sT[:, q % 2, :], turn_bank(("s", q, 0))[0:JE, :], ACT.Copy).then_inc(turn_out, 1)
                    if q + 1 < NQ:
                        sums(q + 1)
                    act.wait_ge(smax_ready, q + 1)
                    if q >= 2:
                        act.wait_ge(turned, turn_at["e", q - 2, 0] + 1)
                        act.wait_ge(added, Q * (q - 1))
                    for i in range(Q):
                        last = act.activation(ex[:, q % 2, i, :], sc[:, q % 2, i, :], ACT.Exp,
                                              bias=smaxn[:, q % 2, i:i + 1], accum_out=rsum[:, q % 2, i:i + 1])
                    last.then_inc(exped, 1)

        def attention_pool(pool):
            own = Tally(pool_own)

            def first_deviations(q):
                s = q % 2
                pool.wait_ge(squares_done, q + 1)
                own.mark(pool.tensor_scalar(norm1[:, s, 0, :], xvar[:, s, :], 1.0 / D, EPS, ALU.mult, ALU.add))
                pool.wait_ge(pool_own, own.n)
                pool.tensor_tensor(norm1[:, s, 1, :], norm1[:, s, 0, :], powers[:, :], ALU.pow).then_inc(normed1, 1)

            def second_deviations(q):
                mv, nm, s = mv2, norm2, q % 2
                own.mark(pool.tensor_scalar(nm[:, s, 0, :], mv[:, s, :, 1], EPS, None, ALU.add))
                own.mark(pool.tensor_scalar(nm[:, s, 1, :], mv[:, s, :, 0], -1.0, None, ALU.mult))
                pool.wait_ge(pool_own, own.n)
                pool.tensor_tensor(nm[:, s, 2, :], nm[:, s, 0, :], powers[:, :], ALU.pow).then_inc(deviated2, 1)
                pool.wait_ge(deviated2, q + 1)
                own.mark(pool.tensor_tensor(nm[:, s, 3, :], nm[:, s, 1, :], nm[:, s, 2, :], ALU.mult))
                pool.wait_ge(pool_own, own.n)

            def mask_biases(q):
                if q == 0:
                    pool.wait_ge(mask_in, 16)
                    wait_evacuated(pool, step_at["cb", 0])
                wait(pool, sc_ready, q - 1)
                wait(pool, mask_ready, q)
                own.mark(pool.tensor_scalar(mflag[:, :, :], mask_i[:, Q * q:Q * q + Q, :], 0.0, MASKED,
                                            ALU.is_equal, ALU.mult))
                pool.wait_ge(pool_own, own.n)
                pool.tensor_tensor(mbias[:, q % 2, :, :], mflag[:, :, :],
                                   cb[:, q // QB, :].unsqueeze(1).to_broadcast([P, Q, J]), ALU.add)\
                    .then_inc(mask_ready, 1)

            mask_biases(0)
            first_deviations(0)
            for it in range(NQ + 1):
                if it + 1 < NQ:
                    mask_biases(it + 1)
                if it == NQ:
                    for f in range(2):
                        weight_low_pool(pool, 0, f)
                    for c in range(NC):
                        gather_pool(pool, 0, 0, c)
                if it == 0:
                    first_deviations(1)
                q = it - 1
                if q >= 0:
                    pool.wait_ge(x1_stats, q + 1)
                    if q >= 2:
                        pool.wait_ge(logit_out, q - 1)
                        pool.wait_ge(xn_out[q % 2], 16 * (q // 2))
                    second_deviations(q)
                    for i in range(Q):
                        if i == Q // 2 and it + 1 < NQ:
                            first_deviations(it + 1)
                        pool.tensor_scalar(xn2[:, q % 2, i, :], x1[:, q % 2, i, :], norm2[:, q % 2, 2, i:i + 1],
                                           norm2[:, q % 2, 3, i:i + 1], ALU.mult, ALU.add).then_inc(normed2, 1)

        def attention_dve(dve, own, between):
            def step(ins):
                own.mark(ins)
                dve.wait_ge(dve_own, own.n)

            def logits_out(q):
                s = q % 2
                dve.wait_ge(routed, q + 1)
                step(dve.tensor_tensor(lg1[:, 0, :, :], VG_BANK[:, 0:Q * E].rearrange("p (i e) -> p i e", i=Q),
                                       rinv[:, s, :].unsqueeze(2).to_broadcast([P, Q, E]), ALU.mult))
                step(dve.tensor_tensor(lg1[:, 1, :, :], lg1[:, 0, :, :], xg1[:, s, :, :], ALU.add))
                dve.wait_ge(deviated2, q + 1)
                dve.tensor_tensor(logits[:, q // QB, (q % QB) * Q:(q % QB) * Q + Q, :], lg1[:, 1, :, :],
                                  norm2[:, s, 2, :].unsqueeze(2).to_broadcast([P, Q, E]), ALU.mult)\
                   .then_inc(logit_out, 1)

            def weigh(q, i):
                n = Q * q + i
                if i == 0:
                    dve.wait_ge(exped, q + 1)
                    step(dve.reciprocal(rinv[:, q % 2, :], rsum[:, q % 2, :]))
                    if q >= 2:
                        dve.wait_ge(x1_out[q % 2], 16 * (q // 2))
                        dve.wait_ge(normed2, Q * (q - 1))
                dve.wait_ge(weighed, n + 1)
                dve.scalar_tensor_tensor(out=x1[:, q % 2, i, :], in0=O_BANKS[n % 2][:, :],
                                         scalar=rinv[:, q % 2, i:i + 1], in1=x_s[:, q % 3, i, :],
                                         op0=ALU.mult, op1=ALU.add).then_inc(added, 1)

            for it in range(NQ + 1):
                if it >= 2:
                    logits_out(it - 2)
                between(it, 0)
                if 0 <= it - 1 < NQ:
                    for i in (0, 1):
                        weigh(it - 1, i)
                q = it
                if q < NQ:
                    bk = SC_BANK[:, 0:Q * JE].rearrange("p (i j) -> p i j", i=Q)
                    dve.wait_ge(scored, q + 1)
                    dve.wait_ge(normed1, q + 1)
                    dve.wait_ge(mask_ready, q + 1)
                    if q >= 1:
                        dve.wait_ge(exped, q)
                    for i in range(Q):
                        last = dve.scalar_tensor_tensor(out=sc[:, q % 2, i, :], in0=bk[:, i, 0:J],
                                                        scalar=norm1[:, q % 2, 1, i:i + 1],
                                                        in1=mbias[:, q % 2, i, :], op0=ALU.mult, op1=ALU.add)
                        own.mark(last) if i < Q - 1 else last.then_inc(sc_ready, 1)
                    dve.wait_ge(sc_ready, q + 1)
                    own.mark(dve.tensor_copy(xg1[:, q % 2, :, :], bk[:, :, J:JE]))
                    dve.wait_ge(dve_own, own.n)
                    step(dve.tensor_reduce(smax[:, q % 2, :], sc[:, q % 2, :, :], AX.X, ALU.max))
                    dve.tensor_scalar(smaxn[:, q % 2, :], smax[:, q % 2, :], -1.0, None, ALU.mult)\
                       .then_inc(smax_ready, 1)
                q = it - 1
                if 0 <= q < NQ:
                    for i in range(2, Q):
                        weigh(q, i)
                between(it, 1)
                if it == NQ:
                    hot_dve(dve, 0, 0, 0)
                    slots_dve(dve, 0, 0, 0)
                if 0 <= q < NQ:
                    if q >= 1:
                        dve.wait_ge(x1_stats, q)
                    for i in range(Q):
                        dve.wait_ge(added, Q * q + i + 1)
                        own.mark(dve.bn_stats(st2[:, i, :], x1[:, q % 2, i, :]))
                    dve.wait_ge(dve_own, own.n)
                    for i in range(Q):
                        last = dve.bn_aggr(mv2[:, q % 2, i, :], st2[:, i, :])
                        own.mark(last) if i < Q - 1 else last.then_inc(x1_stats, 1)
                between(it, 2)
            for c in (0, 1):
                split_tokens_dve(dve, 0, 0, c)
            logits_out(NQ - 1)

        def attention_over(eng):
            eng.wait_ge(logit_out, NQ)
            for i in range(2):
                eng.wait_ge(x1_out[i], 16 * (NQ // 2))
                eng.wait_ge(xn_out[i], 16 * (NQ // 2))

        NE = TB * E
        N_PIECES = STEPS + 2

        def flat(t):
            return t[:, :, :].rearrange("p t e -> p (t e)")

        def over_tiles(t):
            return t.unsqueeze(1).to_broadcast([P, TB, E])

        def tile_counts(dve, dst, flags):
            with nc.allow_low_precision(reason="counts up to 16"):
                return dve.tensor_reduce(dst, flags, AX.X, ALU.add)

        def choice_act(act, b):
            act.wait_ge(pdiff, b + 1)
            act.activation(flat(pexp), flat(prob), ACT.Exp).then_inc(pexped, 1)

        def choice_start_dve(dve, own, b):
            dve.wait_ge(logit_out, QB * (b + 1))
            lg = logits[:, b, :, :]
            own.mark(dve.tensor_reduce(pstat[:, 0, :], lg, AX.X, ALU.max))
            dve.wait_ge(dve_own, own.n)
            dve.tensor_tensor(prob[:, :, :], lg, pstat[:, 0, :].unsqueeze(2).to_broadcast([P, TB, E]),
                              ALU.subtract).then_inc(pdiff, 1)

        def choice_dve(dve, own, b, piece):
            def step(ins):
                own.mark(ins)
                dve.wait_ge(dve_own, own.n)

            if b == 0 and piece == 0:
                choice_start_dve(dve, own, 0)
            if piece == 0:
                own.mark(dve.memset(found[:, 0, CANDS, :], 0.0))
                dve.wait_ge(pexped, b + 1)
                step(dve.tensor_reduce(pstat[:, 1, :], pexp[:, :, :], AX.X, ALU.add))
                step(dve.reciprocal(pstat[:, 2, :], pstat[:, 1, :]))
                step(dve.tensor_tensor(prob[:, :, :], pexp[:, :, :],
                                       pstat[:, 2, :].unsqueeze(2).to_broadcast([P, TB, E]), ALU.mult))
            if 1 <= piece <= STEPS:
                s = piece - 1
                dve.wait_ge(bit_total, b * STEPS + s + 1)
                step(dve.scalar_tensor_tensor(out=found[:, s % 2, 0:CANDS, :],
                                              in0=CHOICE_BANK[:, 0:CANDS * E].rearrange("p (c e) -> p c e", c=CANDS),
                                              scalar=float(CAP), in1=cand[:, :, :].bitcast(F32),
                                              op0=ALU.is_ge, op1=ALU.mult))
                step(dve.tensor_reduce(found[:, 1 - s % 2, CANDS, :], found[:, s % 2, :, :].rearrange("p c e -> p e c"),
                                       AX.X, ALU.max))
            thr = found[:, STEPS % 2, CANDS, :]
            if piece < STEPS:
                s = piece
                step(dve.tensor_tensor(cand[:, :, :], bit_table[:, s, :, :].to_broadcast([P, CANDS, E]),
                                       found[:, s % 2, CANDS, :].bitcast(I32).unsqueeze(1)
                                       .to_broadcast([P, CANDS, E]),
                                       ALU.bitwise_or))
                reach = dve.tensor_tensor(atleast[:, :, :, :],
                                          prob[:, :, :].unsqueeze(1).to_broadcast([P, CANDS, TB, E]),
                                          cand[:, :, :].bitcast(F32).unsqueeze(2).to_broadcast([P, CANDS, TB, E]),
                                          ALU.is_ge)
                if b == 0:
                    reach.then_inc(bit_count, 1)
                else:
                    step(reach)
                if b == 1:
                    tile_counts(dve, count[:, :, :], atleast[:, :, :, :].rearrange("p c t e -> p c e t"))\
                        .then_inc(bit_count, 1)
            elif piece == STEPS:
                dve.tensor_tensor(above[:, :, :], prob[:, :, :], over_tiles(thr), ALU.is_gt).then_inc(pick_in, 1)
                dve.tensor_tensor(tied[:, :, :], prob[:, :, :], over_tiles(thr), ALU.is_equal).then_inc(pick_in, 1)
                dve.wait_ge(pick_in, 3 * b + 1)
                tile_counts(dve, count[:, 0, :], above[:, :, :].rearrange("p t e -> p e t")).then_inc(pick_in, 1)
                dve.wait_ge(pick_in, 3 * b + 3)
                vals = values[:, b, :, :, :]
                step(dve.tensor_scalar(prob[:, :, :], prob[:, :, :], gates[:, 1:2], None, ALU.mult))
                step(dve.tensor_copy(vals[:, :, :, 2], prob[:, :, :]))
                step(dve.tensor_tensor(pexp[:, :, :], prob[:, :, :], vals[:, :, :, 2], ALU.subtract))
                step(dve.tensor_copy(vals[:, :, :, 3], pexp[:, :, :]))
                own.mark(dve.tensor_tensor(vals[:, :, :, 4], pexp[:, :, :], vals[:, :, :, 3], ALU.subtract))
            elif piece == STEPS + 1:
                dve.wait_ge(pick_sum, b + 1)
                tied_before = CHOICE_BANK[:, 0:NE].rearrange("p (t e) -> p t e", t=TB)
                above_before = CHOICE_BANK[:, NE:2 * NE].rearrange("p (t e) -> p t e", t=TB)
                step(dve.tensor_scalar(need[:, :], CHOICE_BANK[:, 2 * NE:2 * NE + E], -1.0, float(CAP), ALU.mult,
                                       ALU.add))
                own.mark(dve.tensor_tensor(tied_taken[:, :, :], tied_before, over_tiles(need[:, :]), ALU.min))
                step(dve.tensor_tensor(fits[:, :, :], tied_before, over_tiles(need[:, :]), ALU.is_lt))
                own.mark(dve.tensor_tensor(place_i[:, :, :], above_before, tied_taken[:, :, :], ALU.add))
                step(dve.tensor_tensor(fits[:, :, :], fits[:, :, :], tied[:, :, :], ALU.mult))
                own.mark(dve.tensor_scalar(flat(part_i), flat(place_i), P - 1, None, ALU.bitwise_and))
                own.mark(dve.tensor_scalar(flat(block_i), flat(place_i), 7, None, ALU.logical_shift_right))
                step(dve.tensor_tensor(chosen[:, :, :], above[:, :, :], fits[:, :, :], ALU.add))
                own.mark(dve.tensor_copy(slot_lo[:, b, :, :], part_i[:, :, :]))
                step(dve.scalar_tensor_tensor(out=slot_hi[:, b, :, :], in0=block_i[:, :, :], scalar=1.0,
                                              in1=chosen[:, :, :], op0=ALU.add, op1=ALU.mult))

        def running_place(pe, flags, at):
            d, f = CHOICE_BANK[:, at:at + NE], flat(flags)
            for s in range(1, TB):
                pe.matmul(d[:, s * E:], ones_m[:, :], f[:, 0:(TB - s) * E], start=(s == 1), stop=False,
                          skip_group_check=True)
            return pe.matmul(d, below_m[:, :], f, start=False, stop=True, skip_group_check=True)

        def choice_pe(pe, b, piece):
            if piece < STEPS:
                if b == 0 and piece == 0:
                    pe.wait_ge(consts, CONSTS)
                pe.wait_ge(bit_count, b * STEPS + piece + 1)
                total = CHOICE_BANK[:, 0:CANDS * E]
                if b == 0:
                    for t in range(TB):
                        last = pe.matmul(total.rearrange("p (c e) -> p c e", c=CANDS), ones_m[:, :],
                                         atleast[:, :, t, :],
                                         start=(t == 0), stop=(t == TB - 1))
                else:
                    last = pe.matmul(total, ones_m[:, :], count[:, :, :].rearrange("p c e -> p (c e)"),
                                     start=True, stop=True)
                last.then_inc(bit_total, 1)
            elif piece == STEPS:
                pe.wait_ge(pick_in, 3 * b + 1)
                running_place(pe, above, NE)
                pe.wait_ge(pick_in, 3 * b + 2)
                running_place(pe, tied, 0)
                pe.wait_ge(pick_in, 3 * b + 3)
                pe.matmul(CHOICE_BANK[:, 2 * NE:2 * NE + E], ones_m[:, :], count[:, 0, :], start=True, stop=True)\
                  .then_inc(pick_sum, 1)

        def beside_attention(do):
            def between(it, place):
                at = (it - CHOOSE_FROM) * PLACES + place
                if it == NQ and place > 0:
                    pieces = range(at, N_PIECES) if place == 1 else ()
                else:
                    pieces = range(at, at + 1) if 0 <= at < N_PIECES else ()
                for piece in pieces:
                    do(0, piece)
            return between

        H_BANKS = (bank[4], bank[5])
        Y_BANKS = (bank[0], bank[1], bank[2], bank[3])
        X_BANKS, SLOT_BANK = (bank[6], bank[7]), bank[7]
        LAG = 2
        AHEAD = 3

        def hidden_pe(pe, e, b, f, inside=None):
            n = e * 2 * KF + b * KF + f
            if f == 0:
                pe.wait_ge(x_split, (e * 2 + b + 1) * NC)
            if b == 0:
                pe.wait_ge(w1_low, e * KF + f + 1)
            wait(pe, h_act, n - 1)
            for k in range(KD):
                for part, xpart in ((W1_HIGH, xTh), (W1_HIGH, xTl), (W1_LOW, xTh)):
                    last = pe.matmul(H_BANKS[f % 2][:, :], weights[:, f, part, k * P:(k + 1) * P],
                                     xpart[:, b, k, :],
                                     start=(k == 0 and part == W1_HIGH and xpart is xTh),
                                     stop=(k == KD - 1 and part == W1_LOW))
                if k == 1 and inside is not None:
                    choice_pe(pe, 1, inside)
            last.then_inc(h_sum, 1)

        def output_pe(pe, e, b, f, inside=None):
            n = e * 2 * KF + b * KF + f
            pe.wait_ge(h_split, n + 1)
            if b == 0:
                pe.wait_ge(w2_low, e * KF + f + 1)
            if f == 0:
                wait(pe, y_act, (e * 2 + b) * 2)
                wait(pe, y_dve, (e * 2 + b) * 2)
            for c in range(NC):
                for hpart, part in ((hh, W2_HIGH), (hh, W2_LOW), (hl, W2_HIGH)):
                    last = pe.matmul(Y_BANKS[c][:, :], hpart[:, f % 2, c * P:(c + 1) * P], weights[:, f, part, :],
                                     start=(f == 0 and hpart is hh and part == W2_HIGH),
                                     stop=(f == KF - 1 and hpart is hl))
                if c == 0 and inside is not None:
                    choice_pe(pe, 1, inside)
                if f == KF - 1 and c < NC - 1:
                    last.then_inc(y_chunk, 1)
            last.then_inc(y_sum, 1)

        def slots_pe(pe, g):
            pe.wait_ge(hot, g + 1)
            for t in range(TB):
                last = pe.matmul(SLOT_BANK[:, 0:NC * NV], onehot[:, t, :],
                                 carried[:, t, :, :].rearrange("p c v -> p (c v)"),
                                 start=(t == 0), stop=(t == TB - 1))
            last.then_inc(slots_sum, 1)

        def tokens_pe(pe, g, c):
            pe.wait_ge(gathered[c], (g + 1) * 16)
            wait(pe, x_split, g * NC + c - 1)
            for k in range(KD):
                last = pe.transpose(X_BANKS[c % 2][:, k * P:(k + 1) * P], xg[:, c, k * P:(k + 1) * P], ident[:, :])
            last.then_inc(x_turned, 1)

        def hot_dve(dve, g, e, b):
            wait(dve, slots_sum, g)
            lo = slot_lo[:, b, :, bass.ds(e, 1)] if not isinstance(e, int) else slot_lo[:, b, :, e:e + 1]
            hi = slot_hi[:, b, :, bass.ds(e, 1)] if not isinstance(e, int) else slot_hi[:, b, :, e:e + 1]
            va = values[:, b, :, bass.ds(e, 1), :] if not isinstance(e, int) else values[:, b, :, e:e + 1, :]
            dve.tensor_tensor(onehot[:, :, :], iota_slot[:, :].unsqueeze(1).to_broadcast([P, TB, P]),
                              lo.to_broadcast([P, TB, P]), ALU.is_equal)
            dve.tensor_tensor(blockhot[:, :, :], iota_block[:, :].unsqueeze(1).to_broadcast([P, TB, NC]),
                              hi.to_broadcast([P, TB, NC]), ALU.is_equal).then_inc(slots_own, 1)
            dve.wait_ge(slots_own, g * 4 + 1)
            dve.tensor_tensor(carried[:, :, :, :], blockhot[:, :, :].unsqueeze(3).to_broadcast([P, TB, NC, NV]),
                              va.to_broadcast([P, TB, NC, NV]), ALU.mult).then_inc(hot, 1)

        def slots_dve(dve, g, e, b):
            dve.wait_ge(slots_sum, g + 1)
            dve.tensor_copy(got[:, :, :], SLOT_BANK[:, 0:NC * NV].rearrange("p (c v) -> p c v", c=NC))\
               .then_inc(slots_own, 1)
            dve.wait_ge(slots_own, g * 4 + 2)
            dve.tensor_tensor(slot_gate[:, b, 0, :], got[:, :, 3], got[:, :, 4], ALU.add).then_inc(slots_own, 1)
            dve.wait_ge(slots_own, g * 4 + 3)
            dve.tensor_tensor(slot_gate[:, b, 1, :], got[:, :, 2], slot_gate[:, b, 0, :], ALU.add)\
               .then_inc(slots_own, 1)
            for c in range(NC):
                wait(dve, scattered[c], (g - 1) * 16)
            row = dve.scalar_tensor_tensor(out=slot_row[:, b, :], in0=got[:, :, 0], scalar=float(P),
                                           in1=got[:, :, 1], op0=ALU.mult, op1=ALU.add)
            if b == 0:
                row.then_inc(slots_ready, 1)
            else:
                row.then_inc(row_ready, 1)
                dve.wait_ge(row_ready, e + 1)
                dve.tensor_scalar(slot_source[:, :], slot_row[:, b, :], float(-b * S), None, ALU.add)\
                   .then_inc(slots_ready, 1)

        def first_tokens_act(act, c):
            act.wait_ge(x_turned, c + 1)
            act.activation(xTh[:, 0, :, c * P:(c + 1) * P],
                           X_BANKS[c % 2][:, :].rearrange("p (k t) -> p k t", k=KD), ACT.Copy).then_inc(x_high, 1)

        def split_tokens_dve(dve, g, b, c):
            src = X_BANKS[c % 2][:, :].rearrange("p (k t) -> p k t", k=KD)
            high, low = xTh[:, b, :, c * P:(c + 1) * P], xTl[:, b, :, c * P:(c + 1) * P]
            if not (isinstance(g, int) and g == 0):
                dve.wait_ge(x_turned, g * NC + c + 1)
                dve.tensor_copy(high, src).then_inc(x_high, 1)
            dve.wait_ge(x_high, g * NC + c + 1)
            dve.tensor_tensor(low, src, high.bitcast(F32), ALU.subtract).then_inc(x_split, 1)

        def split_hidden_dve(dve, e, b, f):
            n = e * 2 * KF + b * KF + f
            dve.wait_ge(h_act, n + 1)
            wait(dve, y_sum, n - 1)
            dve.tensor_copy(hh[:, f % 2, :], hf[:, f % 2, :]).then_inc(h_high, 1)
            dve.wait_ge(h_high, n + 1)
            dve.tensor_tensor(hl[:, f % 2, :], hf[:, f % 2, :], hh[:, f % 2, :].bitcast(F32), ALU.subtract)\
               .then_inc(h_split, 1)

        def gelu_act(act, e, b, f):
            n = e * 2 * KF + b * KF + f
            act.wait_ge(h_sum, n + 1)
            wait(act, h_split, n - 1)
            act.activation(hf[:, f % 2, :], H_BANKS[f % 2][:, :], ACT.Gelu).then_inc(h_act, 1)

        def output_rows(eng, e, b, c, done):
            g = e * 2 + b
            if c < NC - 1:
                eng.wait_ge(y_chunk, g * (NC - 1) + c + 1)
            else:
                eng.wait_ge(y_sum, e * 2 * KF + (b + 1) * KF)
            wait(eng, scattered[c], g * 16)
            gate = slot_gate[:, b, 1, c:c + 1]
            if eng is nc.scalar:
                ins = eng.activation(y[:, c, :], Y_BANKS[c][:, :], ACT.Copy, scale=gate)
            else:
                ins = eng.tensor_scalar(y[:, c, :], Y_BANKS[c][:, :], gate, None, ALU.mult)
            ins.then_inc(done, 1)

        def weight_high_act(act, e, f):
            n = e * KF + f
            used = (e - 1) * 2 * KF + KF + f + 1
            wait(act, h_sum, used)
            wait(act, y_sum, used)
            act.wait_ge(w1_in[f % 2], e * (KF // 2) * 16 + (f // 2 + 1) * 16)
            act.activation(weights[:, f, W1_HIGH, :], raw1[:, f % 2, :, :].rearrange("p k f -> p (k f)"),
                           ACT.Copy).then_inc(w1_high, 1)
            act.wait_ge(w2_in[f % 2], e * (KF // 2) * 16 + (f // 2 + 1) * 16)
            act.activation(weights[:, f, W2_HIGH, :], raw2[:, f % 2, :], ACT.Copy).then_inc(w2_high, 1)

        def weight_low_pool(pool, e, f):
            n = e * KF + f
            pool.wait_ge(w1_high, n + 1)
            pool.tensor_tensor(weights[:, f, W1_LOW, :], raw1[:, f % 2, :, :].rearrange("p k f -> p (k f)"),
                               weights[:, f, W1_HIGH, :].bitcast(F32), ALU.subtract)\
                .then_inc(w1_low, 1)
            pool.wait_ge(w2_high, n + 1)
            pool.tensor_tensor(weights[:, f, W2_LOW, :], raw2[:, f % 2, :], weights[:, f, W2_HIGH, :].bitcast(F32),
                               ALU.subtract)\
                .then_inc(w2_low, 1)

        def gather_pool(pool, g, b, c):
            pool.wait_ge(slots_ready, g + 1)
            wait(pool, x_turned, (g - 1) * NC + c + 1)
            if isinstance(g, int) and g == 0:
                for i in range(2):
                    pool.wait_ge(xn_out[i], 16 * (QB // 2))
            pool.sem_inc(gathers, 1)
            source = slot_row[:, 0, c:c + 1] if b == 0 else slot_source[:, c:c + 1]
            pool.indirect_dma_start(xg[:, c, :], None, xn_rows[b],
                                    bass.IndirectOffsetOnAxis(ap=source, axis=0))\
                .then_inc(gathered[c], 16)

        def scatter_pool(pool, e, b, c):
            g = e * 2 + b
            done, at = (y_act, c) if c < 2 else (y_dve, c - 2)
            pool.wait_ge(done, g * 2 + at + 1)
            for other in range(NC):
                wait(pool, scattered[other], g * 16)
            pool.sem_inc(scatters, 1)
            pool.indirect_dma_start(out_rows, bass.IndirectOffsetOnAxis(ap=slot_row[:, b, c:c + 1], axis=0),
                                    y[:, c, :], None, compute_op=ALU.add).then_inc(scattered[c], 16)

        USUAL = (1, 3, (4, 6, 8, 10), (6, 8, 10, 12))
        FIRST = (11, 12, (12, 12, 12, 12), (14, 14, 15, 15))

        def next_group(e, b):
            return (e, 1) if b == 0 else (e + 1, 0)

        def very_first(e, b):
            return isinstance(e, int) and e == 0 and b == 0

        def choice_piece(e, b, f):
            return f if very_first(e, b) and 1 <= f < N_PIECES else None

        def plan(e, b):
            return FIRST if very_first(e, b) else USUAL

        def new_weights(e, b, f, final):
            if isinstance(e, int) and e == 0 and b == 0:
                return [(0, f + AHEAD)] if f + AHEAD < KF else []
            if b == 0 and f < LAG and not (isinstance(e, int) and e == 0):
                return [(e, KF - LAG + f)]
            if b == 1 and f >= LAG and not final:
                return [(e + 1, f - LAG)]
            return []

        def expert_pe(pe, e, final):
            for b in range(B):
                end = final and b == B - 1
                ne, nb = next_group(e, b)
                g = e * 2 + b + 1
                hot_at, slots_at, gather_at, turn_at_f = plan(e, b)
                for f in range(KF):
                    if f + 1 < KF:
                        hidden_pe(pe, e, b, f + 1, 0 if very_first(e, b) and f == 0 else None)
                    if not end and f == slots_at:
                        slots_pe(pe, g)
                    for c in range(NC):
                        if not end and turn_at_f[c] == f:
                            tokens_pe(pe, g, c)
                    if f + 1 == KF and not end and not very_first(e, b):
                        hidden_pe(pe, ne, nb, 0)
                    output_pe(pe, e, b, f, choice_piece(e, b, f))
                    if f + 1 == KF and very_first(e, b):
                        hidden_pe(pe, ne, nb, 0)

        def expert_dve(dve, own, e, final):
            for b in range(B):
                end = final and b == B - 1
                ne, nb = next_group(e, b)
                g = e * 2 + b + 1
                hot_at, slots_at, gather_at, turn_at_f = plan(e, b)
                for f in range(KF):
                    if choice_piece(e, b, f) is not None:
                        choice_dve(dve, own, 1, choice_piece(e, b, f))
                    if f + 1 < KF:
                        split_hidden_dve(dve, e, b, f + 1)
                    if not end:
                        if f == hot_at:
                            hot_dve(dve, g, ne, nb)
                        if f == slots_at:
                            slots_dve(dve, g, ne, nb)
                        for c in range(NC):
                            if turn_at_f[c] == f:
                                split_tokens_dve(dve, g, nb, c)
                    if f + 1 == KF and not end:
                        split_hidden_dve(dve, ne, nb, 0)
                for c in (2, 3):
                    output_rows(dve, e, b, c, y_dve)

        def expert_act(act, e, final):
            for b in range(B):
                end = final and b == B - 1
                ne, nb = next_group(e, b)
                for f in range(KF):
                    if f + 1 < KF:
                        gelu_act(act, e, b, f + 1)
                    elif not end:
                        gelu_act(act, ne, nb, 0)
                    for chunk in new_weights(e, b, f, final):
                        weight_high_act(act, *chunk)
                for c in (0, 1):
                    output_rows(act, e, b, c, y_act)

        def expert_pool(pool, e, final):
            for b in range(B):
                end = final and b == B - 1
                ne, nb = next_group(e, b)
                g = e * 2 + b + 1
                hot_at, slots_at, gather_at, turn_at_f = plan(e, b)
                for f in range(KF):
                    for chunk in new_weights(e, b, f, final):
                        weight_low_pool(pool, *chunk)
                    for c in range(NC):
                        if not end and gather_at[c] == f:
                            gather_pool(pool, g, nb, c)
                for c in range(NC):
                    scatter_pool(pool, e, b, c)

        def load_weights(sp, e, f):
            n = e * KF + f
            wait(sp, w1_low, n - 1)
            sp.dma_start(raw1[:, f % 2, :, :], w1_v[e, :, :, f * P:(f + 1) * P] if isinstance(e, int) else
                         w1_v[bass.ds(e, 1), :, :, f * P:(f + 1) * P].rearrange("o p k f -> (o p) k f"))\
              .then_inc(w1_in[f % 2], 16)
            wait(sp, w2_low, n - 1)
            sp.dma_start(raw2[:, f % 2, :], w2_v[e, :, f, :] if isinstance(e, int) else
                         w2_v[bass.ds(e, 1), :, f, :].rearrange("o p d -> (o p) d"))\
              .then_inc(w2_in[f % 2], 16)

        CONSTS = 5 + CANDS

        @block.sync
        def _(sp):
            small = [(bias_rows[0:KD, :], bk.rearrange("(c p) -> c p", p=P)),
                     (bias_rows[KD:2 * KD, :], bv.rearrange("(c p) -> c p", p=P)),
                     (bias_rows[2 * KD:3 * KD, :], bq.rearrange("(c p) -> c p", p=P)),
                     (bo_all[:, :], bo.rearrange("(a d) -> a d", a=1).to_broadcast([J, D])),
                     (gate_raw[:, :], gate_w)]
            sp.dma_start(raw_k[:, :, :], Wk.rearrange("(c p) e -> p c e", p=P)).then_inc(lin[2], 16)
            for dst, src in small:
                sp.dma_start(dst, src).then_inc(lin[0], 16)
            sp.dma_start(ctx_raw[:, :, :], ctx_in.rearrange("b j d -> j b d")).then_inc(lin[1], 16)
            sp.dma_start(x_s[:, 0, :, :], x_q[0]).then_inc(x_in[0], 16)
            sp.dma_start(raw_q[:, :, :], Wq.rearrange("(c p) e -> p c e", p=P)).then_inc(lin[3], 16)
            sp.dma_start(raw_v[:, :, :], Wv.rearrange("(c p) e -> p c e", p=P)).then_inc(lin[4], 16)
            sp.dma_start(x_s[:, 1, :, :], x_q[1]).then_inc(x_in[1], 16)
            sp.dma_start(raw_o[:, :, :], Wo.rearrange("(c p) e -> p c e", p=P)).then_inc(lin[5], 16)
            sp.dma_start(mask_i[:, :, :], mask_v).then_inc(mask_in, 16)
            sp.dma_start(x_s[:, 2, :, :], x_q[2]).then_inc(x_in[2], 16)
            for q in range(NQ):
                if q + 1 == NQ:
                    for f in (2, 3):
                        load_weights(sp, 0, f)
                sp.wait_ge(added, Q * q + Q)
                if q + 3 < NQ:
                    sp.dma_start(x_s[:, q % 3, :, :], x_q[q + 3]).then_inc(x_in[q % 3], 16)
                elif q + 3 < NQ + 2:
                    load_weights(sp, 0, q + 3 - NQ)
                sp.dma_start(out_q[q], x1[:, q % 2, :, :]).then_inc(x1_out[q % 2], 16)
                sp.wait_ge(normed2, Q * q + Q)
                sp.dma_start(xn_q[q // QB][q % QB], xn2[:, q % 2, :, :]).then_inc(xn_out[q % 2], 16)
            for f in range(4, KF):
                load_weights(sp, 0, f)
            with sp.Fori(1, E) as e:
                for f in range(KF):
                    load_weights(sp, e, f)
            for c in range(NC):
                sp.wait_ge(scattered[c], 16 * G)

        @block.gpsimd
        def _(pool):
            pool.dma_start(gates_raw[:, 0:1], g_xattn.rearrange("(a o) -> a o", o=1).to_broadcast([P, 1]))\
                .then_inc(lin[6], 16)
            pool.dma_start(gates_raw[:, 1:2], g_ffn.rearrange("(a o) -> a o", o=1).to_broadcast([P, 1]))\
                .then_inc(lin[6], 16)
            pool.memset(ident[:, :], 0.0).then_inc(pool_start, 1)
            pool.memset(powers[:, :], -0.5).then_inc(pool_start, 1)
            pool.memset(vo[:, :, :], 0.0).then_inc(pool_start, 1)
            pool.memset(vg[:, :, :], 0.0).then_inc(pool_start, 1)
            pool.wait_ge(pool_start, 1)
            pool.affine_select(out=ident[:, :], in_=ident[:, :], compare_op=ALU.not_equal, fill=1.0, base=0,
                               pattern=[[-1, P]], channel_multiplier=1).then_inc(consts, 1)
            pool.memset(mean_m[:, :], 1.0 / D).then_inc(consts, 1)
            pool.wait_ge(pool_start, 4)
            pool.memset(eT[:, :, :], 0.0).then_inc(consts, 1)
            pool.memset(ones_m[:, :], 1.0).then_inc(consts, 1)
            pool.memset(below_m[:, :], 1.0).then_inc(pool_start, 1)
            for c in range(CANDS):
                pool.memset(bit_table[:, 0, c, :], (c + 1) << (BITS - BITS_PER_STEP)).then_inc(consts, 1)
            pool.wait_ge(pool_start, 5)
            pool.affine_select(out=below_m[:, :], in_=below_m[:, :], compare_op=ALU.is_gt, fill=0.0, base=0,
                               pattern=[[1, P]], channel_multiplier=-1).then_inc(consts, 1)
            pool.iota(vrow_i[:, :], pattern=[[1, NT]], base=0, channel_multiplier=0).then_inc(iotas, 1)
            pool.iota(vpar_i[:, :], pattern=[[1, 1]], base=0, channel_multiplier=1).then_inc(iotas, 1)
            pool.iota(iota_i[:, :], pattern=[[1, P]], base=0, channel_multiplier=0).then_inc(iotas, 1)
            attention_pool(pool)
            weight_low_pool(pool, 0, 2)
            attention_over(pool)
            expert_pool(pool, 0, False)
            with pool.Fori(1, E - 1) as e:
                expert_pool(pool, e, False)
            expert_pool(pool, E - 1, True)

        @block.scalar
        def _(act):
            act.wait_ge(lin[6], 32)
            act.activation(gates[:, :], gates_raw[:, :], ACT.Tanh).then_inc(gates_done, 1)
            prep_out(act, prep_act, True)
            attention_act(act)
            act.wait_ge(scored, NQ)
            weight_high_act(act, 0, 2)
            for c in range(NC):
                first_tokens_act(act, c)
            choice_act(act, 1)
            act.activation(spare_gate[:, :], gates[:, 0:1], ACT.Gelu)
            act.wait_ge(added, Q * NQ)
            gelu_act(act, 0, 0, 0)
            attention_over(act)
            expert_act(act, 0, False)
            with act.Fori(1, E - 1) as e:
                expert_act(act, e, False)
            expert_act(act, E - 1, True)

        @block.vector
        def _(dve):
            own = Tally(dve_own)
            prep_out(dve, prep_dve, False)
            dve.wait_ge(iotas, 3)
            for b in range(B):
                own.mark(dve.tensor_copy(values[:, b, :, :, 0],
                                         vrow_i[:, b * TB:(b + 1) * TB].unsqueeze(2).to_broadcast([P, TB, E])))
                own.mark(dve.tensor_copy(values[:, b, :, :, 1],
                                         vpar_i[:, 0:1].unsqueeze(2).to_broadcast([P, TB, E])))
            own.mark(dve.tensor_copy(iota_slot[:, :], iota_i[:, :]))
            own.mark(dve.tensor_scalar(iota_block[:, :], iota_i[:, 0:NC], 1.0, None, ALU.add))
            dve.wait_ge(consts, CONSTS)
            for s in range(1, STEPS):
                own.mark(dve.tensor_scalar(bit_table[:, s, :, :], bit_table[:, 0, :, :], BITS_PER_STEP * s, None,
                                           ALU.logical_shift_right))
            attention_dve(dve, own, beside_attention(lambda b, n: choice_dve(dve, own, b, n)))
            choice_start_dve(dve, own, 1)
            for c in (2, 3):
                split_tokens_dve(dve, 0, 0, c)
            choice_dve(dve, own, 1, 0)
            split_hidden_dve(dve, 0, 0, 0)
            expert_dve(dve, own, 0, False)
            with dve.Fori(1, E - 1) as e:
                expert_dve(dve, None, e, False)
            expert_dve(dve, None, E - 1, True)

        @block.tensor
        def _(pe):
            prep_pe(pe)
            attention_pe(pe, beside_attention(lambda b, n: choice_pe(pe, b, n)))
            slots_pe(pe, 0)
            for c in range(NC):
                tokens_pe(pe, 0, c)
            hidden_pe(pe, 0, 0, 0)
            pe.wait_ge(logit_out, NQ)
            expert_pe(pe, 0, False)
            with pe.Fori(1, E - 1) as e:
                expert_pe(pe, e, False)
            expert_pe(pe, E - 1, True)


INPUTS = ["x", "ctx_1024", "mask_BxSxS2_ik0", "g_xattn", "g_ffn", "L0_xattn_Wq", "L0_xattn_bq", "L0_xattn_Wk",
          "L0_xattn_bk", "L0_xattn_Wv", "L0_xattn_bv", "L0_xattn_Wo", "L0_xattn_bo", "L0_ffn_gate_w", "L0_ffn_w1",
          "L0_ffn_w2"]


def kernel(**inputs):
    import concourse.bacc as bacc
    from concourse.bass_utils import run_bass_kernel_spmd

    nc = bacc.Bacc("TRN2", target_bir_lowering=False, num_devices=1)
    arrays, args = {}, []
    for name in INPUTS:
        a = np.ascontiguousarray(inputs[name])
        arrays[f"in_{name}"] = a
        args.append(nc.dram_tensor(f"in_{name}", a.shape, mybir.dt.from_np(a.dtype), kind="ExternalInput").ap())
    shape = inputs["x"].shape
    args.append(nc.dram_tensor("layer_out", shape, F32, kind="ExternalOutput").ap())
    flamingo_layer(nc, *args)
    r = run_bass_kernel_spmd(nc, [arrays], core_ids=[0])
    return r.results[0]["layer_out"]
```
